# Optimizing a Trainium2 kernel written in Bass

```python
import numpy as np
import jax
import jax.numpy as jnp

def _softmax(x, axis=-1):
    return jax.nn.softmax(x, axis=axis)

def _gelu(x):
    return jax.nn.gelu(x, approximate=True)

def _silu(x):
    return jax.nn.silu(x)

def _sigmoid(x):
    return jax.nn.sigmoid(x)

def _layernorm(x, axis=-1, eps=1e-05):
    m = jnp.mean(x, axis=axis, keepdims=True)
    v = jnp.var(x, axis=axis, keepdims=True)
    return (x - m) / jnp.sqrt(v + eps)

def _scatter_add(tgt, idx, src, axis=0):
    return tgt.at[idx].add(src)

def _segment_sum(src, seg, n):
    return jax.ops.segment_sum(src, seg, n)
kernel_name = 'mk_gnn_resnorm_d2_gnn_r8_94ab34'

def setup_inputs(seed: int=0):
    np.random.seed(seed)
    _w = jnp.asarray

    def _rec_inputs():
        import jax
        import jax.numpy as jnp
        _gk = jax.random.key(seed)
        x = -0.000202 + 1 * jax.random.normal(jax.random.fold_in(_gk, 1), (6250, 128), jnp.float32)
        src = jax.random.randint(jax.random.fold_in(_gk, 2), (100000,), 0, 6250, jnp.int32)
        dst = jnp.minimum((6250 * jax.random.uniform(jax.random.fold_in(_gk, 3), (100000,)) ** 2.0).astype(jnp.int32), 49999)
        _o = jnp.argsort(dst, stable=True)
        src = src[_o]
        dst = dst[_o]
        edge_type_32 = jax.random.randint(jax.random.fold_in(_gk, 12), (100000,), 0, 32, jnp.int32)
        edge_weight1 = jax.random.uniform(jax.random.fold_in(_gk, 13), (100000, 1), jnp.float32, 0.0, 0.999998)
        return (x, src, dst, edge_type_32, edge_weight1)
    x, src, dst, edge_type_32, edge_weight1 = _rec_inputs()

    def _L0_gnn_setup():
        import jax, jax.numpy as jnp
        import numpy as np
        N, E, D, F, R, B = (6250, 200000, 128, 128, 32, 8)
        key = jax.random.key(seed)
        ks = jax.random.split(key, 9)
        h = jax.random.normal(ks[0], (N, D), dtype=jnp.float32)
        src = jax.random.randint(ks[1], (E,), 0, N, dtype=jnp.int32)
        dst = jax.random.randint(ks[2], (E,), 0, N, dtype=jnp.int32)
        etype = jax.random.randint(ks[3], (E,), 0, R, dtype=jnp.int32)
        norm = jax.random.uniform(ks[4], (E, 1), dtype=jnp.float32)
        weight = jax.random.normal(ks[5], (B, D, F), dtype=jnp.float32) * (2.0 / (D + F)) ** 0.5
        w_comp = jax.random.normal(ks[6], (R, B), dtype=jnp.float32) * (2.0 / (R + B)) ** 0.5
        loop_weight = jax.random.normal(ks[7], (D, F), dtype=jnp.float32) * (2.0 / (D + F)) ** 0.5
        h_bias = jnp.zeros((F,), dtype=jnp.float32)
        return {'h': h, 'src': src, 'dst': dst, 'etype': etype, 'norm': norm, 'weight': weight, 'w_comp': w_comp, 'loop_weight': loop_weight, 'h_bias': h_bias}
    _L0_gnn_all = _L0_gnn_setup()
    _L0_gnn_in = {k: v for k, v in _L0_gnn_all.items() if k in ('weight', 'w_comp', 'loop_weight', 'h_bias')}
    del _L0_gnn_all

    def _L1_gnn_setup():
        import jax, jax.numpy as jnp
        import numpy as np
        N, E, C = (12500, 200000, 128)
        EPS = 1e-05

        def _bn(x, g, b):
            mu = jnp.mean(x, axis=0)
            var = jnp.mean((x - mu) ** 2, axis=0)
            return g * (x - mu) * jax.lax.rsqrt(var + EPS) + b
        key = jax.random.key(seed)
        ks = jax.random.split(key, 8)
        s = 1.0 / np.sqrt(C)
        return {'h': jax.random.normal(ks[0], (N, C), jnp.float32), 'src': jax.random.randint(ks[1], (E,), 0, N, jnp.int32), 'dst': jax.random.randint(ks[2], (E,), 0, N, jnp.int32), 'theta_w': jax.random.normal(ks[3], (C, C), jnp.float32) * s, 'phi_w': jax.random.normal(ks[4], (C, C), jnp.float32) * s, 'fc1_w': jax.random.normal(ks[5], (C, C), jnp.float32) * s, 'bn0_g': jnp.ones((C,), jnp.float32), 'bn0_b': jnp.zeros((C,), jnp.float32), 'bn1_g': jnp.ones((C,), jnp.float32), 'bn1_b': jnp.zeros((C,), jnp.float32)}
    _L1_gnn_all = _L1_gnn_setup()
    _L1_gnn_in = {k: v for k, v in _L1_gnn_all.items() if k in ('theta_w', 'phi_w', 'fc1_w', 'bn0_g', 'bn0_b', 'bn1_g', 'bn1_b')}
    del _L1_gnn_all
    return {'x': x, 'src': src, 'dst': dst, 'edge_type_32': edge_type_32, 'edge_weight1': edge_weight1, 'L0_gnn_weight': _L0_gnn_in['weight'], 'L0_gnn_w_comp': _L0_gnn_in['w_comp'], 'L0_gnn_loop_weight': _L0_gnn_in['loop_weight'], 'L0_gnn_h_bias': _L0_gnn_in['h_bias'], 'L1_gnn_theta_w': _L1_gnn_in['theta_w'], 'L1_gnn_phi_w': _L1_gnn_in['phi_w'], 'L1_gnn_fc1_w': _L1_gnn_in['fc1_w'], 'L1_gnn_bn0_g': _L1_gnn_in['bn0_g'], 'L1_gnn_bn0_b': _L1_gnn_in['bn0_b'], 'L1_gnn_bn1_g': _L1_gnn_in['bn1_g'], 'L1_gnn_bn1_b': _L1_gnn_in['bn1_b']}

def reference(x, src, dst, edge_type_32, edge_weight1, L0_gnn_weight, L0_gnn_w_comp, L0_gnn_loop_weight, L0_gnn_h_bias, L1_gnn_theta_w, L1_gnn_phi_w, L1_gnn_fc1_w, L1_gnn_bn0_g, L1_gnn_bn0_b, L1_gnn_bn1_g, L1_gnn_bn1_b):
    import jax
    import jax.numpy as jnp

    def _L0_gnn_ref(h, src, dst, etype, norm, weight, w_comp, loop_weight, h_bias):
        import jax, jax.numpy as jnp
        import numpy as np
        N, E, D, F, R, B = (6250, 200000, 128, 128, 32, 8)
        n_nodes, d_in = h.shape
        n_rels = w_comp.shape[0]
        W_rel = jnp.einsum('rb,bdf->rdf', w_comp, weight)
        seg = etype * n_nodes + dst
        agg = jax.ops.segment_sum(h[src] * norm, seg, num_segments=n_rels * n_nodes)
        agg = agg.reshape(n_rels, n_nodes, d_in)
        node_repr = jnp.einsum('rnd,rdf->nf', agg, W_rel)
        node_repr = node_repr + h_bias + h @ loop_weight
        return jax.nn.relu(node_repr)

    def _L1_gnn_ref(h, src, dst, theta_w, phi_w, fc1_w, bn0_g, bn0_b, bn1_g, bn1_b):
        import jax, jax.numpy as jnp
        import numpy as np
        N, E, C = (12500, 200000, 128)
        EPS = 1e-05

        def _bn(x, g, b):
            mu = jnp.mean(x, axis=0)
            var = jnp.mean((x - mu) ** 2, axis=0)
            return g * (x - mu) * jax.lax.rsqrt(var + EPS) + b
        n = h.shape[0]
        x_src = h[src]
        x_dst = h[dst]
        e = (x_dst - x_src) @ theta_w.T + x_src @ phi_w.T
        e = jax.nn.relu(_bn(e, bn0_g, bn0_b))
        e = e @ fc1_w.T
        e = jax.nn.relu(_bn(e, bn1_g, bn1_b))
        agg = jax.ops.segment_sum(e, dst, num_segments=n)
        cnt = jax.ops.segment_sum(jnp.ones((e.shape[0],), e.dtype), dst, num_segments=n)
        x = agg / jnp.maximum(cnt, 1.0)[:, None]
        return jax.nn.relu(x + h)
    x = _layernorm(x + _L0_gnn_ref(x, src, dst, edge_type_32, edge_weight1, L0_gnn_weight, L0_gnn_w_comp, L0_gnn_loop_weight, L0_gnn_h_bias), axis=-1)
    x = _layernorm(x + _L1_gnn_ref(x, src, dst, L1_gnn_theta_w, L1_gnn_phi_w, L1_gnn_fc1_w, L1_gnn_bn0_g, L1_gnn_bn0_b, L1_gnn_bn1_g, L1_gnn_bn1_b), axis=-1)
    return x

_drawn_inputs = setup_inputs


def setup_inputs(seed=0):
    import zlib

    import numpy as np

    out = dict(_drawn_inputs(seed))
    spreads = {'L0_gnn_h_bias': (0.0, 0.1),
     'L1_gnn_bn0_g': (1.0, 0.537),
     'L1_gnn_bn0_b': (0.0, 0.635),
     'L1_gnn_bn1_g': (1.0, 0.2),
     'L1_gnn_bn1_b': (0.0, 0.331)}
    factors = {}
    for name, (base, spread) in spreads.items():
        noise = np.random.default_rng([zlib.crc32(name.encode()), seed]).standard_normal(out[name].shape)
        drawn = base * np.exp(spread * noise) if base else spread * noise
        out[name] = jnp.asarray(drawn.astype(out[name].dtype))
    for name, factor in factors.items():
        out[name] = (out[name] * factor).astype(out[name].dtype)
    return out
```

```python
from contextlib import ExitStack

import concourse.bass as bass
from concourse import mybir

P = 128
F32 = mybir.dt.float32
BF16 = mybir.dt.bfloat16
I32 = mybir.dt.int32
ALU = mybir.AluOpType
ACT = mybir.ActivationFunctionType
AX = mybir.AxisListType
EPS = 1e-5

D = 128
TILE = 128
TPC = 4
CHUNK = TILE * TPC
CPG = 4
TPG = TPC * CPG
GROUP = CHUNK * CPG
WIN = 128


def take(eng, sem, n=1):
    eng.wait_ge(sem, n)
    eng.sem_inc(sem, -n)


def gnn_kernel(nc, x, src, dst, etype, norm, weight, w_comp, loop_w, h_bias,
               theta, phi, fc1, g0, b0, g1, b1, out):
    N = x.shape[0]
    E = src.shape[0]
    R, B = w_comp.shape
    NW = (N + WIN - 1) // WIN
    LASTN = N - (NW - 1) * WIN
    NG = (E + GROUP - 1) // GROUP
    NCH = NG * CPG
    NB = (NG * TPG + P - 1) // P
    FULLB = E // (P * TILE)
    LROWS = E // TILE - FULLB * P
    LEDGE = E % TILE
    LASTC = E - (NCH - 1) * CHUNK
    PAIRS = NG // 2
    RW = R * D
    assert NG % 2 == 1 and 0 < LASTC <= CHUNK and FULLB == NB - 1 and LEDGE

    ctx = ExitStack()

    def sb(name, shape, dt=F32):
        return ctx.enter_context(nc.sbuf_tensor(name, shape, dt))

    def sem(name):
        return ctx.enter_context(nc.semaphore(name))

    with ctx:
        table = nc.dram_tensor("table", [NW * WIN * R, D], F32, kind="Internal").ap()
        wrel_d = nc.dram_tensor("wrel_d", [R, D * D], F32, kind="Internal").ap()
        btab = nc.dram_tensor("btab", [NW * WIN, D], F32, kind="Internal").ap()
        digits_d = nc.dram_tensor("digits_d", [2, NB * P * TILE], BF16, kind="Internal").ap()
        bounds_d = nc.dram_tensor("bounds_d", [NB, 2 * P // TPC], I32, kind="Internal").ap()
        spill = nc.dram_tensor("spill", [NG, P, GROUP], F32, kind="Internal").ap()

        X = sb("X", [P, NW, D])
        ACC = sb("ACC", [P, NW, D + 1])
        iota_n = sb("iota_n", [P, NW * WIN])
        node_col = sb("node_col", [P, NW])
        ident = sb("ident", [P, P])
        ones = sb("ones", [P, P])
        ones2 = sb("ones2", [2, P], BF16)
        idx0T = sb("idx0T", [P, NB * P], I32)
        srcT = sb("srcT", [P, NB * P], I32)
        dstT = sb("dstT", [P, NB * P])
        normT = sb("normT", [P, NB * P])
        bounds = sb("bounds", [1, NB * 2 * P // TPC], I32)
        ix = sb("ix", [P, 2, TPG], I32)
        G = sb("G", [P, 2, TPG, D])
        oh = sb("oh", [P, TPC, WIN])
        ohT = sb("ohT", [P, CHUNK], BF16)
        digits = sb("digits", [2, 2, GROUP], BF16)
        stage = sb("stage", [P, 2, GROUP])
        small = sb("small", [P, 64])
        theta_s = sb("theta_s", [P, D])
        phi_s = sb("phi_s", [P, D])
        fc1_s = sb("fc1_s", [P, D])
        thph = sb("thph", [P, 2 * D])
        fc1T = sb("fc1T", [P, D])
        fc1sT = sb("fc1sT", [P, D])
        negt = sb("negt", [P, D])
        diag = sb("diag", [P, D])
        loop_s = sb("loop_s", [P, D])
        bias_b = sb("bias_b", [P, D])
        bn_in = sb("bn_in", [P, 4])
        stats = sb("stats", [P, NCH, 6])
        ln_st = sb("ln_st", [P, NW, 6])
        ln_mv = sb("ln_mv", [P, NW, 2])
        ln_r = sb("ln_r", [P, NW])
        bst = sb("bst", [P, 2, D])
        xn = sb("xn", [P, 2, D])
        xT = sb("xT", [P, 2, D])
        resid = sb("resid", [P, D])
        BIG = sb("BIG", [P, 3 * RW])
        tout = BIG[:, 0:2 * RW].rearrange("p (s n) -> p s n", s=2)
        wrel = BIG[:, 2 * RW:3 * RW]
        wst = tout[0:B, 0, :].rearrange("p (s n) -> p s n", s=2)
        ost = tout[0:R, 1, :].rearrange("p (s n) -> p s n", s=2)
        EB = NB * TILE

        accf = ACC[:, :, :].rearrange("p w d -> p (w d)")
        r_src = accf[:, 0:EB].bitcast(I32).rearrange("p (b e) -> p b e", b=NB)
        r_typ = accf[:, EB:2 * EB].bitcast(I32).rearrange("p (b e) -> p b e", b=NB)
        r_dst = accf[:, 2 * EB:3 * EB].bitcast(I32).rearrange("p (b e) -> p b e", b=NB)
        r_nrm = accf[:, 3 * EB:4 * EB].rearrange("p (b e) -> p b e", b=NB)
        f_idx = accf[:, 4 * EB:5 * EB].rearrange("p (b e) -> p b e", b=NB)
        f_src = accf[:, 5 * EB:6 * EB].rearrange("p (b e) -> p b e", b=NB)
        f_dst = accf[:, 6 * EB:7 * EB].rearrange("p (b e) -> p b e", b=NB)
        stgf = stage[:, :, :].rearrange("p s n -> p (s n)")
        i_hi = stgf[:, 0:EB].bitcast(I32).rearrange("p (b e) -> p b e", b=NB)
        f_min = stgf[:, EB:2 * EB].rearrange("p (b e) -> p b e", b=NB)
        dig_hi = stgf[:, 2 * EB:2 * EB + EB // 2].bitcast(BF16).rearrange("p (b e) -> p b e", b=NB)
        dig_lo = stgf[:, 2 * EB + EB // 2:3 * EB].bitcast(BF16).rearrange("p (b e) -> p b e", b=NB)
        t_min = stgf[:, 3 * EB:3 * EB + NB]
        t_max = stgf[:, 3 * EB + NB:3 * EB + 2 * NB]
        NK = P // TPC
        c_bnd = stgf[0:NB, 3 * EB + 64:3 * EB + 64 + 2 * NK]
        c_int = stgf[0:NB, 3 * EB + 192:3 * EB + 192 + 2 * NK].bitcast(I32)
        c_win = stgf[0:NB, 3 * EB + 320:3 * EB + 320 + 2 * NK].bitcast(I32)
        A3 = BIG[:, 0:3 * NW * D // 2].bitcast(BF16).rearrange("p (a w d) -> p a w d", a=3, w=NW)
        hot = BIG[:, 0:2 * GROUP].rearrange("p (s n) -> p s n", s=2)
        R2 = BIG[:, 2 * GROUP:2 * GROUP + 2 * TPC * (D + 1)].rearrange("p (s q d) -> p s q d", s=2, q=TPC)

        PS = ctx.enter_context(nc.psum_tensor("PS", [P, 8, 512], F32))

        const_done = sem("const_done")
        pads_set = sem("pads_set")
        x_in = sem("x_in")
        edges_in = sem("edges_in")
        wts_in = sem("wts_in")
        wcomp_in = sem("wcomp_in")
        wst_in = [sem("wst_in0"), sem("wst_in1")]
        wst_used = sem("wst_used")
        ost_ready = sem("ost_ready")
        ost_out = [sem("ost_out0"), sem("ost_out1")]
        wrel_ps = sem("wrel_ps")
        wrel_ps_free = sem("wrel_ps_free")
        wrel_in = sem("wrel_in")
        dve_self = sem("dve_self")
        act_self = sem("act_self")
        rows_f = sem("rows_f")
        digits_ready = sem("digits_ready")
        digits_out = sem("digits_out")
        minmax = sem("minmax")
        minmax_T = sem("minmax_T")
        bnd_ready = sem("bnd_ready")
        bnd_out = sem("bnd_out")
        bnd_in = sem("bnd_in")
        rows_T = sem("rows_T")
        cols_ready = sem("cols_ready")
        wT_ps = sem("wT_ps")
        wT_done = sem("wT_done")
        xwin_ready = sem("xwin_ready")
        xwin_free = sem("xwin_free")
        xwT_ps = sem("xwT_ps")
        xwT_ready = sem("xwT_ready")
        tab_ps = sem("tab_ps")
        tab_ps_dve = sem("tab_ps_dve")
        tab_free_act = sem("tab_free_act")
        tab_free_dve = sem("tab_free_dve")
        loop_ps = sem("loop_ps")
        loop_done = sem("loop_done")
        tout_act = sem("tout_act")
        tout_dve = sem("tout_dve")
        tout_out = [sem("tout_out0"), sem("tout_out1")]
        tout_free_act = sem("tout_free_act")
        tout_free_dve = sem("tout_free_dve")
        table_done = sem("table_done")
        ix_ready = sem("ix_ready")
        ix_free = sem("ix_free")
        gathered = [sem(f"gathered{i}") for i in range(2 * CPG)]
        g_free = sem("g_free")
        oh_ready = sem("oh_ready")
        seg_ready = sem("seg_ready")
        seg_free = sem("seg_free")
        ticks = {e: sem(f"tick_{e}") for e in ("pe", "act", "sp", "pool", "dve")}
        var_ready = sem("var_ready")
        sd_ready = sem("sd_ready")
        xn_ready = sem("xn_ready")
        xn_kept = sem("xn_kept")
        xn_free = sem("xn_free")
        nT_ps = sem("nT_ps")
        nT_ready = sem("nT_ready")
        a_ps = sem("a_ps")
        b_ps = sem("b_ps")
        b_copied = sem("b_copied")
        a_split = sem("a_split")
        bst_ready = sem("bst_ready")
        bst_out = [sem("bst_out0"), sem("bst_out1")]
        btab_done = sem("btab_done")
        dig_in = [sem("dig_in0"), sem("dig_in1")]
        dig_free = sem("dig_free")
        d_ready = sem("d_ready")
        d_free = sem("d_free")
        ohT_ready = sem("ohT_ready")
        look_done = sem("look_done")
        e_ready = sem("e_ready")
        e_free = sem("e_free")
        e_copied = sem("e_copied")
        e_measured = sem("e_measured")
        stored = [sem("stored0"), sem("stored1")]
        bn0_ready = sem("bn0_ready")
        st_in = [sem("st_in0"), sem("st_in1")]
        st_free = sem("st_free")
        hot_ready = sem("hot_ready")
        hot_free = sem("hot_free")
        e2_ready = sem("e2_ready")
        e2_free = sem("e2_free")
        pass2_read = sem("pass2_read")
        bn_var = sem("bn_var")
        bn_sd = sem("bn_sd")
        fc1_scaled = sem("fc1_scaled")
        fc1s_ps = sem("fc1s_ps")
        pass3_go = sem("pass3_go")
        y_ready = sem("y_ready")
        y_free = sem("y_free")
        r2_ready = sem("r2_ready")
        res_ready = sem("res_ready")
        out_done = sem("out_done")

        def reached(eng, name, s, value):
            eng.wait_ge(s, value)
            eng.sem_inc(ticks[name], 1)

        def pairwise(eng, body):
            body(0, 0, 0)
            body(1, 1, 0)
            with eng.Fori(1, PAIRS) as i:
                body(2 * i, 0, i)
                body(2 * i + 1, 1, i)
            body(NG - 1, 0, PAIRS)

        def window_pairs(eng, body):
            body(0, 0, 0)
            body(1, 1, 0)
            with eng.Fori(1, NW // 2) as i:
                body(2 * i, 0, i)
                body(2 * i + 1, 1, i)
            body(NW - 1, 0, NW // 2)

        def chunk_windows(eng, c):
            lo = eng.value_load(bounds[0:1, bass.ds(c * 2, 1)], min_val=0, max_val=NW - 1)
            hi = eng.value_load(bounds[0:1, bass.ds(c * 2 + 1, 1)], min_val=1, max_val=NW)
            return lo, hi

        def edge_rows(a):
            return a[0:FULLB * P * TILE].rearrange("(b p e) -> p b e", p=P, e=TILE)

        block = ctx.enter_context(nc.Block())

        @block.sync
        def _(sp):
            sp.wait_ge(pads_set, 5)
            norm_v = norm.rearrange("e o -> (e o)")
            last = FULLB * P * TILE
            for vec, r in ((src, r_src), (etype, r_typ), (dst, r_dst), (norm_v, r_nrm)):
                sp.dma_start(r[:, 0:FULLB, :], edge_rows(vec)).then_inc(edges_in, 16)
                sp.dma_start(r[0:LROWS, FULLB, :],
                             vec[last:last + LROWS * TILE].rearrange("(p e) -> p e", e=TILE)).then_inc(edges_in, 16)
                sp.dma_start(r[LROWS:LROWS + 1, FULLB, 0:LEDGE],
                             vec[E - LEDGE:E].rearrange("(p e) -> p e", p=1)).then_inc(edges_in, 16)
            wv = weight.rearrange("b d f -> b (d f)")
            n = RW // 2
            pieces = D * D // n
            sp.dma_start(small[0:B, 0:R], w_comp.rearrange("r b -> b r"),
                         allow_slow_non_contiguous=True).then_inc(wcomp_in, 16)
            for s in range(pieces + 1):
                if s < pieces:
                    if s >= 2:
                        sp.wait_ge(wst_used, 4 * (s - 1))
                    sp.dma_start(wst[:, s % 2, :], wv[:, s * n:(s + 1) * n]).then_inc(wst_in[s % 2], 16)
                if s >= 1:
                    take(sp, ost_ready)
                    sp.dma_start(wrel_d[:, (s - 1) * n:s * n], ost[:, (s - 1) % 2, :]).then_inc(ost_out[(s - 1) % 2], 16)
            for a, t in ((loop_s, loop_w), (theta_s, theta), (phi_s, phi), (fc1_s, fc1)):
                sp.dma_start(a[:, :], t).then_inc(wts_in, 16)
            sp.dma_start(bias_b[:, :], h_bias.rearrange("(o f) -> o f", o=1).to_broadcast([P, D])).then_inc(wts_in, 16)
            for k, v in enumerate((g0, b0, g1, b1)):
                sp.dma_start(bn_in[:, k:k + 1], v.rearrange("(f o) -> f o", o=1)).then_inc(wts_in, 16)
            sp.dma_start(X[:, 0:NW - 1, :], x[0:(NW - 1) * WIN, :].rearrange("(w p) d -> p w d", p=P)).then_inc(x_in, 16)
            sp.dma_start(X[0:LASTN, NW - 1, :], x[(NW - 1) * WIN:N, :]).then_inc(x_in, 16)
            for q in range(2):
                sp.wait_ge(ost_out[q], 16 * pieces // 2)
            sp.dma_start(wrel.rearrange("p (r f) -> p r f", r=R),
                         wrel_d.rearrange("r (d f) -> d r f", d=D)).then_inc(wrel_in, 16)
            sp.wait_ge(digits_ready, 1)
            for k, dg in enumerate((dig_hi, dig_lo)):
                sp.dma_start(digits_d[k, :].rearrange("(b p e) -> p b e", p=P, e=TILE), dg).then_inc(digits_out, 16)
            sp.wait_ge(bnd_ready, 1)
            sp.dma_start(bounds_d[:, :], c_win).then_inc(bnd_out, 16)
            sp.wait_ge(bnd_out, 16)
            sp.dma_start(bounds[:, :], bounds_d.rearrange("(o b) c -> o (b c)", o=1)).then_inc(bnd_in, 16)

            def store_table(w, s, use):
                take(sp, tout_act)
                take(sp, tout_dve)
                sp.dma_start(table[bass.ds(w * (WIN * R), WIN * R), :].rearrange("(p r) d -> p (r d)", p=P),
                             tout[:, s, :]).then_inc(tout_out[s], 16)
                if s == 1 or not (isinstance(use, int) and use == 0):
                    reached(sp, "sp", tout_out[1 - s], 16 * (use + s))
                    sp.sem_inc(tout_free_act, 1)
                    sp.sem_inc(tout_free_dve, 1)
            window_pairs(sp, store_table)
            sp.wait_ge(tout_out[0], 16 * (NW - NW // 2))
            sp.wait_ge(tout_out[1], 16 * (NW // 2))
            sp.sem_inc(table_done, 1)

            def store_b(w, s, use):
                take(sp, bst_ready)
                sp.dma_start(btab[bass.ds(w * WIN, WIN), :], bst[:, s, :]).then_inc(bst_out[s], 16)
            window_pairs(sp, store_b)
            sp.wait_ge(bst_out[0], 16 * (NW - NW // 2))
            sp.wait_ge(bst_out[1], 16 * (NW // 2))
            sp.sem_inc(btab_done, 1)

            sp.wait_ge(digits_out, 32)

            def load_digits(g, h, use):
                take(sp, dig_free)
                sp.dma_start(digits[:, h, :], digits_d[:, bass.ds(g * GROUP, GROUP)]).then_inc(dig_in[h], 16)
            pairwise(sp, load_digits)

            sp.wait_ge(stored[0], 16 * (PAIRS + 1))
            sp.wait_ge(stored[1], 16 * PAIRS)
            for base in range(2):
                def load_e(g, h, use):
                    take(sp, st_free)
                    sp.dma_start(stage[:, h, :], spill[bass.ds(g, 1), :, :].rearrange("o p n -> (o p) n")).then_inc(st_in[h], 16)
                take(sp, st_free, 2)
                sp.sem_inc(st_free, 2)
                pairwise(sp, load_e)

            def store_out(w, s, use):
                take(sp, res_ready)
                if isinstance(w, int) and w == NW - 1:
                    sp.dma_start(out[w * WIN:N, :], xn[0:LASTN, s, :]).then_inc(bst_out[s], 16)
                else:
                    sp.dma_start(out[bass.ds(w * WIN, WIN), :], xn[:, s, :]).then_inc(bst_out[s], 16)
            window_pairs(sp, store_out)
            sp.wait_ge(bst_out[0], 32 * (NW - NW // 2))
            sp.wait_ge(bst_out[1], 32 * (NW // 2))

        @block.gpsimd
        def _(pool):
            nc.gpsimd.memset(r_src[:, FULLB, :], 0).then_inc(pads_set, 1)
            nc.gpsimd.memset(r_typ[:, FULLB, :], 0).then_inc(pads_set, 1)
            nc.gpsimd.memset(r_dst[:, FULLB, :], -1).then_inc(pads_set, 1)
            nc.gpsimd.memset(X[:, NW - 1, :], 0.0).then_inc(pads_set, 1)
            nc.gpsimd.memset(r_nrm[:, FULLB, :], 0.0).then_inc(pads_set, 1)
            nc.gpsimd.memset(ones[:, :], 1.0).then_inc(const_done, 1)
            nc.gpsimd.memset(ones2[:, :], 1.0).then_inc(const_done, 1)
            nc.gpsimd.memset(ident[:, :], 0.0).then_inc(const_done, 1)
            pool.wait_ge(const_done, 3)
            nc.gpsimd.affine_select(out=ident[:, :], in_=ident[:, :], compare_op=ALU.not_equal, fill=1.0, base=0,
                                    pattern=[[-1, P]], channel_multiplier=1).then_inc(const_done, 1)
            nc.gpsimd.iota(iota_n[:, :], pattern=[[1, NW * WIN]], base=0, channel_multiplier=0,
                           allow_small_or_imprecise_dtypes=True).then_inc(const_done, 1)
            nc.gpsimd.iota(node_col[:, :], pattern=[[WIN, NW]], base=0, channel_multiplier=1,
                           allow_small_or_imprecise_dtypes=True).then_inc(const_done, 1)
            pool.sem_inc(g_free, 2 * CPG)
            pool.sem_inc(ix_free, 2)

            def gathers(rows_of):
                def one(g, h, use):
                    take(pool, ix_ready)
                    for k in range(CPG):
                        take(pool, g_free)
                        for q in range(TPC):
                            t = TPC * k + q
                            nc.gpsimd.indirect_dma_start(
                                out=G[:, h, t, :], out_offset=None, in_=rows_of,
                                in_offset=bass.IndirectOffsetOnAxis(ap=ix[:, h, t:t + 1], axis=0),
                            ).then_inc(gathered[CPG * h + k], 16)
                pairwise(pool, one)

            pool.wait_ge(table_done, 1)
            gathers(table[:, :])

            def keep(w, s, use):
                take(pool, xn_kept)
                nc.gpsimd.tensor_copy(X[:, bass.ds(w, 1), :].rearrange("p o d -> p (o d)"), xn[:, s, :]).then_inc(xn_free, 1)
            window_pairs(pool, keep)

            pool.wait_ge(btab_done, 1)
            gathers(btab[:, :])

        @block.tensor
        def _(pe):
            pe.wait_ge(const_done, 6)
            pe.wait_ge(wcomp_in, 16)
            n = RW // 2
            for s in range(D * D // n):
                pe.wait_ge(wst_in[s % 2], 16 * (s // 2 + 1))
                if s >= 2:
                    take(pe, wrel_ps_free)
                for j in range(n // 512):
                    pe.matmul(PS[0:R, 4 * (s % 2) + j, :], small[0:B, 0:R], wst[:, s % 2, j * 512:(j + 1) * 512],
                              start=True, stop=True).then_inc(wst_used, 1)
            pe.wait_ge(rows_f, 3)
            pe.wait_ge(wrel_ps_free, 2)
            for k, f in enumerate((f_idx, f_src, f_dst, r_nrm)):
                for b in range(NB):
                    mm = pe.transpose(PS[:, 2 * k + b // 4, (b % 4) * P:(b % 4 + 1) * P], f[:, b, :], ident[:, :])
                mm.then_inc(rows_T, 1)
            pe.wait_ge(cols_ready, 4)
            pe.wait_ge(minmax, 2)
            pe.transpose(PS[0:NB, 0, 0:P], t_min, ident[:, :])
            pe.transpose(PS[0:NB, 0, P:2 * P], t_max, ident[:, :]).then_inc(minmax_T, 1)
            pe.wait_ge(wts_in, 16 * 9)
            pe.transpose(PS[:, 1, 0:D], theta_s[:, :], ident[:, :])
            pe.transpose(PS[:, 1, D:2 * D], phi_s[:, :], ident[:, :])
            pe.transpose(PS[:, 1, 2 * D:3 * D], fc1_s[:, :], ident[:, :]).then_inc(wT_ps, 1)
            pe.wait_ge(wT_done, 1)

            pe.wait_ge(wrel_in, 16)

            def table_rows(w, s, use):
                take(pe, xwin_ready)
                pe.transpose(PS[:, 0, 0:P], xn[:, s, :], ident[:, :]).then_inc(xwT_ps, 1)
                take(pe, xwT_ready)
                take(pe, loop_done)
                pe.matmul(PS[:, 1, 0:D], xT[:, s, :], loop_s[:, :], start=True, stop=True).then_inc(loop_ps, 1)
                for j in range(RW // 512):
                    free, full = ((tab_free_act, tab_ps), (tab_free_dve, tab_ps_dve))[j % 2]
                    take(pe, free)
                    bank = 2 + j % 2 + 2 * ((j // 2) % 2)
                    pe.matmul(PS[:, bank, :], xT[:, s, :], wrel[:, j * 512:(j + 1) * 512],
                              start=True, stop=True).then_inc(full, 1)
            window_pairs(pe, table_rows)

            pe.wait_ge(bnd_in, 16)
            uses = [0]

            def add_messages(g, h, use):
                for k in range(CPG):
                    lo, hi = chunk_windows(pe, CPG * g + k)
                    reached(pe, "pe", gathered[CPG * h + k], 16 * TPC * (use + 1))
                    with pe.Fori(lo, hi):
                        take(pe, seg_free)
                        for q in range(TPC):
                            take(pe, oh_ready)
                            mm = pe.matmul(PS[:, 0, 0:D], oh[:, q, :], G[:, h, TPC * k + q, :],
                                           start=(q == 0), stop=(q == TPC - 1))
                        mm.then_inc(seg_ready, 1)
            pairwise(pe, add_messages)

            def node_tables(w, s, use):
                take(pe, xn_ready)
                pe.transpose(PS[:, 2 + s, 0:P], xn[:, s, :], ident[:, :]).then_inc(nT_ps, 1)
                take(pe, nT_ready)
                take(pe, b_copied)
                take(pe, a_split)
                pe.matmul(PS[:, 4 + s, 0:D], xT[:, s, :], thph[:, 0:D], start=True, stop=True).then_inc(a_ps, 1)
                pe.matmul(PS[:, 6 + s, 0:D], xT[:, s, :], thph[:, D:2 * D], start=True, stop=True).then_inc(b_ps, 1)
            window_pairs(pe, node_tables)

            def edge_features(g, h, use):
                reached(pe, "pe", dig_in[h], 16 * (use + 1))
                for k in range(CPG):
                    take(pe, d_free)
                    pe.matmul(PS[:, k % 2, :], ones2[:, :], digits[:, h, k * CHUNK:(k + 1) * CHUNK],
                              start=True, stop=True).then_inc(d_ready, 1)
                    lo, hi = chunk_windows(pe, CPG * g + k)
                    reached(pe, "pe", gathered[CPG * h + k], 16 * TPC * (use + 1 + (PAIRS + 1 if h == 0 else PAIRS)))
                    take(pe, e_free)
                    for q in range(TPC):
                        pe.matmul(PS[:, 2 + k % 2, q * TILE:(q + 1) * TILE], G[:, h, TPC * k + q, :], ident[:, :],
                                  start=(q == 0), stop=False, skip_group_check=True)
                    with pe.Fori(lo, hi) as w:
                        take(pe, ohT_ready)
                        for a in range(3):
                            mm = pe.matmul(PS[:, 2 + k % 2, :], A3[:, a, bass.ds(w, 1), :].rearrange("p o d -> p (o d)"),
                                           ohT[:, :], start=False, stop=False, skip_group_check=True)
                        mm.then_inc(look_done, 1)
            pairwise(pe, edge_features)

            def second_product(g, h, use):
                take(pe, hot_ready)
                pe.sem_inc(st_free, 1)
                for k in range(CPG):
                    take(pe, e2_free)
                    pe.matmul(PS[:, CPG * h + k, :], fc1T[:, :], hot[:, h, k * CHUNK:(k + 1) * CHUNK],
                              start=True, stop=True).then_inc(e2_ready, 1)
            pairwise(pe, second_product)

            take(pe, fc1_scaled)
            pe.transpose(PS[:, 0, 0:D], diag[:, :], ident[:, :])
            pe.matmul(PS[:, 1, 0:D], ones[:, :], negt[:, :], start=True, stop=True).then_inc(fc1s_ps, 1)
            pe.wait_ge(pass3_go, 1)

            def y_of(h, k):
                take(pe, y_free)
                for q in range(TPC):
                    t = TPC * k + q
                    mm = pe.matmul(PS[:, k % 2, q * D:(q + 1) * D], hot[:, h, t * TILE:(t + 1) * TILE], fc1sT[:, :],
                                   start=(q == 0), stop=(q == TPC - 1), skip_group_check=True)
                mm.then_inc(y_ready, 1)

            def sum_edges(g, h, use):
                take(pe, hot_ready)
                pe.sem_inc(st_free, 1)
                for k in range(CPG):
                    if k == 0:
                        y_of(h, 0)
                    if k + 1 < CPG:
                        y_of(h, k + 1)
                    lo, hi = chunk_windows(pe, CPG * g + k)
                    take(pe, r2_ready)
                    with pe.Fori(lo, hi):
                        take(pe, seg_free)
                        for q in range(TPC):
                            take(pe, oh_ready)
                            mm = pe.matmul(PS[:, 2, 0:D + 1], oh[:, q, :], R2[:, k % 2, q, :],
                                           start=(q == 0), stop=(q == TPC - 1))
                        mm.then_inc(seg_ready, 1)
            pairwise(pe, sum_edges)

        @block.scalar
        def _(act):
            act.wait_ge(const_done, 6)
            n = RW // 2
            for s in range(D * D // n):
                act.wait_ge(wst_used, 4 * (s + 1))
                if s >= 2:
                    act.wait_ge(ost_out[s % 2], 16 * (s // 2))
                act.activation(ost[:, s % 2, :], PS[0:R, 4 * (s % 2):4 * (s % 2) + 4, :].rearrange("p b n -> p (b n)"),
                               ACT.Copy).then_inc(act_self, 1)
                take(act, act_self)
                act.sem_inc(wrel_ps_free, 1)
                act.sem_inc(ost_ready, 1)
            act.sem_inc(tab_free_act, 2)

            def table_half(w, s, use):
                take(act, xwT_ps)
                act.activation(xT[:, s, :], PS[:, 0, 0:P], ACT.Copy).then_inc(xwT_ready, 1)
                take(act, tout_free_act)
                for j in range(0, RW // 512, 2):
                    take(act, tab_ps)
                    bank = 2 + 2 * ((j // 2) % 2)
                    ins = act.activation(tout[:, s, j * 512:(j + 1) * 512], PS[:, bank, :], ACT.Copy)
                    ins.then_inc(tab_free_act, 1)
                act.drain().then_inc(tout_act, 1)
            act.wait_ge(wT_done, 1)
            window_pairs(act, table_half)

            def indices(of):
                def one(g, h, use):
                    take(act, ix_free)
                    act.activation(ix[:, h, :], of[:, bass.ds(g * TPG, TPG)], ACT.Copy).then_inc(ix_ready, 1)
                pairwise(act, one)

            act.wait_ge(cols_ready, 4)
            indices(idx0T)

            take(act, var_ready)
            act.activation(ln_r[:, :], ln_mv[:, :, 1], ACT.Sqrt).then_inc(sd_ready, 1)

            def copy_b(w, s, use):
                take(act, nT_ps)
                act.activation(xT[:, s, :], PS[:, 2 + s, 0:P], ACT.Copy).then_inc(nT_ready, 1)
                take(act, b_ps)
                if not (isinstance(use, int) and use == 0):
                    reached(act, "act", bst_out[s], 16 * use)
                act.activation(bst[:, s, :], PS[:, 6 + s, 0:D], ACT.Copy).then_inc(act_self, 1)
                take(act, act_self)
                act.sem_inc(bst_ready, 1)
                act.sem_inc(b_copied, 1)
            act.sem_inc(b_copied, 2)
            window_pairs(act, copy_b)

            take(act, ix_free)
            act.activation(ix[:, 0, :], srcT[:, 0:TPG], ACT.Copy).then_inc(ix_ready, 1)
            take(act, ix_free)
            act.activation(ix[:, 1, :], srcT[:, TPG:2 * TPG], ACT.Copy).then_inc(ix_ready, 1)
            act.sem_inc(e_free, 2)

            def store_e(g, h, use):
                if not (isinstance(use, int) and use == 0):
                    reached(act, "act", stored[h], 16 * use)
                    take(act, e_measured)
                for k in range(CPG):
                    take(act, e_ready)
                    act.activation(stage[:, h, k * CHUNK:(k + 1) * CHUNK], PS[:, 2 + k % 2, :],
                                   ACT.Copy).then_inc(act_self, 1)
                    take(act, act_self)
                    act.sem_inc(e_free, 1)
                    act.sem_inc(e_copied, 1)
                act.dma_start(spill[bass.ds(g, 1), :, :].rearrange("o p n -> (o p) n"), stage[:, h, :]).then_inc(stored[h], 16)
                if not isinstance(g, int) or g + 2 < NG:
                    take(act, ix_free)
                    act.activation(ix[:, h, :], srcT[:, bass.ds((g + 2) * TPG, TPG)], ACT.Copy).then_inc(ix_ready, 1)

            store_e(0, 0, 0)
            store_e(1, 1, 0)
            with act.Fori(1, PAIRS - 1) as i:
                store_e(2 * i, 0, i)
                store_e(2 * i + 1, 1, i)
            for g in range(NG - 3, NG):
                store_e(g, g % 2, g // 2)
            take(act, e_measured, 2)

            act.sem_inc(st_free, 2)
            act.sem_inc(hot_free, 2)
            for at, go, before in ((0, bn0_ready, (0, 0)), (8, pass3_go, (PAIRS + 1, PAIRS))):
                take(act, bn_var)
                act.activation(small[:, at + 3:at + 4], small[:, at + 2:at + 3], ACT.Sqrt).then_inc(bn_sd, 1)
                act.wait_ge(go, 1)

                def relu_e(g, h, use, before=before):
                    reached(act, "act", st_in[h], 16 * (use + 1 + before[h]))
                    take(act, hot_free)
                    act.activation(hot[:, h, :], stage[:, h, :], ACT.Relu, bias=small[:, 6:7],
                                   scale=small[:, 5:6]).then_inc(hot_ready, 1)
                pairwise(act, relu_e)

            take(act, var_ready)
            act.activation(ln_r[:, :], ln_mv[:, :, 1], ACT.Sqrt).then_inc(sd_ready, 1)

        @block.vector
        def _(dve):
            def step(ins):
                ins.then_inc(dve_self, 1)
                take(dve, dve_self)

            dve.wait_ge(const_done, 6)
            dve.wait_ge(edges_in, 16 * 12)
            dve.scalar_tensor_tensor(out=f_idx, in0=r_src, scalar=float(R), in1=r_typ, op0=ALU.mult, op1=ALU.add).then_inc(rows_f, 1)
            dve.tensor_copy(f_src, r_src).then_inc(rows_f, 1)
            dve.tensor_copy(f_dst, r_dst).then_inc(rows_f, 1)
            step(dve.tensor_scalar(i_hi, r_dst, 7, None, ALU.arith_shift_right))
            dve.tensor_scalar(dig_hi, i_hi, float(WIN), None, ALU.mult)
            step(dve.scalar_tensor_tensor(out=dig_lo, in0=i_hi, scalar=-float(WIN), in1=r_dst, op0=ALU.mult, op1=ALU.add))
            dve.sem_inc(digits_ready, 1)
            step(dve.tensor_scalar(f_min, f_dst, 0.0, float(1 << 13), ALU.is_lt, ALU.mult))
            step(dve.tensor_tensor(f_min, f_min, f_dst, ALU.add))
            dve.tensor_reduce(t_min, f_min, AX.X, ALU.min).then_inc(minmax, 1)
            dve.tensor_reduce(t_max, f_dst, AX.X, ALU.max).then_inc(minmax, 1)
            for k, to in enumerate((idx0T, srcT, dstT, normT)):
                dve.wait_ge(rows_T, k + 1)
                dve.tensor_copy(to[:, :], PS[:, 2 * k:2 * k + 2, :].rearrange("p b n -> p (b n)")[:, 0:NB * P]).then_inc(cols_ready, 1)
            take(dve, minmax_T)
            for k, op in enumerate((ALU.min, ALU.max)):
                ins = dve.tensor_reduce(c_bnd[:, k:2 * NK:2], PS[0:NB, 0, k * P:(k + 1) * P].rearrange("b (c t) -> b c t", t=TPC), AX.X, op)
                step(ins)
            step(dve.tensor_copy(c_int, c_bnd))
            step(dve.tensor_scalar(c_win, c_int, 7, None, ALU.arith_shift_right))
            step(dve.tensor_scalar(c_win[:, 1:2 * NK:2], c_win[:, 1:2 * NK:2], 1.0, None, ALU.add))
            dve.sem_inc(bnd_ready, 1)
            dve.wait_ge(wT_ps, 1)
            step(dve.tensor_copy(thph[:, 0:D], PS[:, 1, 0:D]))
            step(dve.tensor_copy(fc1T[:, :], PS[:, 1, 2 * D:3 * D]))
            step(dve.tensor_tensor(thph[:, D:2 * D], PS[:, 1, D:2 * D], thph[:, 0:D], ALU.subtract))
            dve.wait_ge(x_in, 32)
            dve.sem_inc(wT_done, 1)
            dve.sem_inc(tab_free_dve, 2)
            dve.sem_inc(tout_free_act, 2)
            dve.sem_inc(tout_free_dve, 2)
            dve.sem_inc(loop_done, 1)

            def table_half(w, s, use):
                dve.tensor_copy(xn[:, s, :], X[:, bass.ds(w, 1), :].rearrange("p o d -> p (o d)")).then_inc(xwin_ready, 1)
                take(dve, loop_ps)
                dve.tensor_tensor(ACC[:, bass.ds(w, 1), 0:D].rearrange("p o d -> p (o d)"), PS[:, 1, 0:D],
                                  bias_b[:, :], ALU.add).then_inc(loop_done, 1)
                take(dve, tout_free_dve)
                for j in range(1, RW // 512, 2):
                    take(dve, tab_ps_dve)
                    bank = 3 + 2 * ((j // 2) % 2)
                    dve.tensor_copy(tout[:, s, j * 512:(j + 1) * 512], PS[:, bank, :]).then_inc(tab_free_dve, 1)
                dve.drain().then_inc(tout_dve, 1)
            window_pairs(dve, table_half)

            dve.wait_ge(bnd_in, 16)
            dve.sem_inc(seg_free, 1)

            def one_hots(w, g, k, scaled):
                for q in range(TPC):
                    t = TPG * g + TPC * k + q
                    dve.tensor_scalar(oh[:, q, :], iota_n[:, bass.ds(w * WIN, WIN)], dstT[:, bass.ds(t, 1)],
                                      normT[:, bass.ds(t, 1)] if scaled else None, ALU.is_equal,
                                      *((ALU.mult,) if scaled else ())).then_inc(oh_ready, 1)

            def add_messages(g, h, use):
                for k in range(CPG):
                    lo, hi = chunk_windows(dve, CPG * g + k)
                    with dve.Fori(lo, hi) as w:
                        one_hots(w, g, k, True)
                        take(dve, seg_ready)
                        acc = ACC[:, bass.ds(w, 1), 0:D].rearrange("p o d -> p (o d)")
                        dve.tensor_tensor(acc, acc, PS[:, 0, 0:D], ALU.add).then_inc(seg_free, 1)
                    dve.sem_inc(g_free, 1)
                dve.sem_inc(ix_free, 1)
            pairwise(dve, add_messages)
            take(dve, seg_free)

            def layer_norm_stats():
                with dve.Fori(0, NW) as w:
                    xw = X[:, bass.ds(w, 1), :].rearrange("p o d -> p (o d)")
                    dve.bn_stats(ln_st[:, bass.ds(w, 1), :].rearrange("p o d -> p (o d)"), xw).then_inc(dve_self, 1)
                dve.wait_ge(dve_self, NW)
                dve.sem_inc(dve_self, -NW)
                m0, m1, v0, v1 = ln_st[:, :, 1], ln_st[:, :, 4], ln_st[:, :, 2], ln_st[:, :, 5]
                step(dve.tensor_tensor(ln_mv[:, :, 0], m0, m1, ALU.add))
                step(dve.tensor_scalar(ln_mv[:, :, 0], ln_mv[:, :, 0], 0.5, None, ALU.mult))
                step(dve.tensor_tensor(ln_mv[:, :, 1], m0, m1, ALU.subtract))
                step(dve.tensor_scalar(ln_mv[:, :, 1], ln_mv[:, :, 1], 0.5, None, ALU.mult))
                step(dve.tensor_tensor(ln_mv[:, :, 1], ln_mv[:, :, 1], ln_mv[:, :, 1], ALU.mult))
                step(dve.tensor_tensor(ln_r[:, :], v0, v1, ALU.add))
                step(dve.scalar_tensor_tensor(out=ln_mv[:, :, 1], in0=ln_r[:, :], scalar=1.0 / D, in1=ln_mv[:, :, 1],
                                              op0=ALU.mult, op1=ALU.add))
                step(dve.tensor_scalar(ln_mv[:, :, 1], ln_mv[:, :, 1], EPS, None, ALU.add))
                dve.sem_inc(var_ready, 1)
                take(dve, sd_ready)
                step(dve.reciprocal(ln_r[:, :], ln_r[:, :]))

            def normalise(w, s):
                return dve.tensor_scalar(xn[:, s, :], X[:, bass.ds(w, 1), :].rearrange("p o d -> p (o d)"),
                                         ln_mv[:, bass.ds(w, 1), 0], ln_r[:, bass.ds(w, 1)], ALU.subtract, ALU.mult)

            step(dve.scalar_tensor_tensor(out=X[:, :, :], in0=ACC[:, :, 0:D], scalar=0.0, in1=X[:, :, :],
                                          op0=ALU.max, op1=ALU.add))
            layer_norm_stats()

            dve.sem_inc(a_split, 2)
            dve.sem_inc(xn_free, 2)

            def node_tables(w, s, use):
                take(dve, xn_free)
                step(normalise(w, s))
                dve.sem_inc(xn_kept, 1)
                dve.sem_inc(xn_ready, 1)
                take(dve, a_ps)
                ps = PS[:, 4 + s, 0:D]
                hi, mid, low = (A3[:, a, bass.ds(w, 1), :].rearrange("p o d -> p (o d)") for a in range(3))
                step(dve.tensor_copy(hi, ps))
                step(dve.tensor_tensor(resid[:, :], ps, hi, ALU.subtract))
                step(dve.tensor_copy(mid, resid[:, :]))
                step(dve.tensor_tensor(low, resid[:, :], mid, ALU.subtract))
                dve.sem_inc(a_split, 1)
            window_pairs(dve, node_tables)
            take(dve, xn_free, 2)

            dve.sem_inc(dig_free, 2)
            dve.sem_inc(d_free, 2)

            def first_moments(g, h, k):
                c = CPG * g + k
                take(dve, e_copied)
                cols = LASTC if isinstance(c, int) and c == NCH - 1 else CHUNK
                dve.bn_stats(stats[:, bass.ds(c, 1), :].rearrange("p o d -> p (o d)"),
                             stage[:, h, k * CHUNK:k * CHUNK + cols])

            def edge_features(g, h, use):
                for k in range(CPG):
                    c = CPG * g + k
                    lo, hi = chunk_windows(dve, c)
                    take(dve, d_ready)
                    with dve.Fori(lo, hi) as w:
                        dve.tensor_scalar(ohT[:, :], PS[:, k % 2, :], node_col[:, bass.ds(w, 1)], None,
                                          ALU.is_equal).then_inc(ohT_ready, 1)
                        take(dve, look_done)
                    dve.sem_inc(d_free, 1)
                    dve.sem_inc(g_free, 1)
                    dve.sem_inc(e_ready, 1)
                    if k >= 1:
                        first_moments(g, h, k - 1)
                first_moments(g, h, CPG - 1)
                dve.drain().then_inc(e_measured, 1)
                dve.sem_inc(dig_free, 1)
                dve.sem_inc(ix_free, 1)
            pairwise(dve, edge_features)

            def scale_and_shift(at, g, b):
                step(dve.bn_aggr(small[:, at + 1:at + 3], stats[:, :, :].rearrange("p c s -> p (c s)")))
                step(dve.tensor_scalar(small[:, at + 2:at + 3], small[:, at + 2:at + 3], EPS, None, ALU.add))
                dve.sem_inc(bn_var, 1)
                take(dve, bn_sd)
                step(dve.reciprocal(small[:, at + 4:at + 5], small[:, at + 3:at + 4]))
                step(dve.tensor_tensor(small[:, at + 5:at + 6], small[:, at + 4:at + 5], bn_in[:, g:g + 1], ALU.mult))
                step(dve.tensor_tensor(small[:, at + 7:at + 8], small[:, at + 1:at + 2], small[:, at + 5:at + 6], ALU.mult))
                step(dve.tensor_tensor(small[:, at + 6:at + 7], bn_in[:, b:b + 1], small[:, at + 7:at + 8], ALU.subtract))

            scale_and_shift(0, 0, 1)
            dve.sem_inc(e2_free, 2 * CPG)
            dve.sem_inc(bn0_ready, 1)

            def second_moments(g, h, use):
                for k in range(CPG):
                    c = CPG * g + k
                    take(dve, e2_ready)
                    cols = LASTC if isinstance(c, int) and c == NCH - 1 else CHUNK
                    dve.bn_stats(stats[:, bass.ds(c, 1), :].rearrange("p o d -> p (o d)"),
                                 PS[:, CPG * h + k, 0:cols]).then_inc(e2_free, 1)
                dve.sem_inc(hot_free, 1)
            pairwise(dve, second_moments)
            dve.wait_ge(e2_free, 2 * CPG)
            scale_and_shift(8, 2, 3)
            step(dve.tensor_scalar(diag[:, :], fc1_s[:, :], small[:, 13:14], None, ALU.mult))
            step(dve.tensor_scalar(negt[:, :], ident[:, :], small[:, 14:15], -1.0, ALU.mult, ALU.mult))
            dve.sem_inc(fc1_scaled, 1)
            take(dve, fc1s_ps)
            step(dve.tensor_copy(fc1sT[:, :], PS[:, 0, 0:D]))
            step(dve.tensor_copy(negt[:, :], PS[:, 1, 0:D]))
            step(dve.memset(ACC[:, :, :], 0.0))
            step(dve.memset(R2[:, :, :, :], 1.0))
            dve.sem_inc(y_free, 2)
            dve.sem_inc(pass3_go, 1)

            def sum_edges(g, h, use):
                for k in range(CPG):
                    take(dve, y_ready)
                    if k == CPG - 1:
                        dve.sem_inc(hot_free, 1)
                    step(dve.tensor_tensor(R2[:, k % 2, :, 0:D], PS[:, k % 2, :].rearrange("p (q d) -> p q d", q=TPC),
                                           negt[:, :].rearrange("p (o d) -> p o d", o=1).to_broadcast([P, TPC, D]), ALU.max))
                    dve.sem_inc(y_free, 1)
                    dve.sem_inc(r2_ready, 1)
                    lo, hi = chunk_windows(dve, CPG * g + k)
                    with dve.Fori(lo, hi) as w:
                        one_hots(w, g, k, False)
                        take(dve, seg_ready)
                        acc = ACC[:, bass.ds(w, 1), :].rearrange("p o d -> p (o d)")
                        dve.tensor_tensor(acc, acc, PS[:, 2, 0:D + 1], ALU.add).then_inc(seg_free, 1)
            dve.sem_inc(seg_free, 1)
            pairwise(dve, sum_edges)
            take(dve, seg_free)

            cnt, rcp = ln_st[:, :, 0], ln_r[:, :]
            step(dve.tensor_copy(cnt, ACC[:, :, D]))
            step(dve.tensor_scalar(ln_st[:, :, 3], cnt, 1.0, None, ALU.max))
            step(dve.reciprocal(rcp, ln_st[:, :, 3]))
            bw = [P, NW, D]
            negt_all = negt[:, :].rearrange("p (o d) -> p o d", o=1).to_broadcast(bw)
            iot = iota_n[:, :].rearrange("p (w d) -> p w d", w=NW)
            step(dve.tensor_tensor(iot, negt_all, cnt.rearrange("p (w o) -> p w o", o=1).to_broadcast(bw), ALU.mult))
            step(dve.tensor_tensor(iot, ACC[:, :, 0:D], iot, ALU.subtract))
            step(dve.tensor_tensor(iot, iot, rcp.rearrange("p (w o) -> p w o", o=1).to_broadcast(bw), ALU.mult))
            step(dve.tensor_tensor(iot, iot, X[:, :, :], ALU.add))
            step(dve.scalar_tensor_tensor(out=X[:, :, :], in0=iot, scalar=0.0, in1=X[:, :, :], op0=ALU.max, op1=ALU.add))
            layer_norm_stats()

            def result(w, s, use):
                if not (isinstance(use, int) and use == 0):
                    reached(dve, "dve", bst_out[s], 16 * (use + (NW - NW // 2 if s == 0 else NW // 2)))
                normalise(w, s).then_inc(res_ready, 1)
            window_pairs(dve, result)


_INS = ['x', 'src', 'dst', 'edge_type_32', 'edge_weight1', 'L0_gnn_weight', 'L0_gnn_w_comp', 'L0_gnn_loop_weight',
        'L0_gnn_h_bias', 'L1_gnn_theta_w', 'L1_gnn_phi_w', 'L1_gnn_fc1_w', 'L1_gnn_bn0_g', 'L1_gnn_bn0_b',
        'L1_gnn_bn1_g', 'L1_gnn_bn1_b']


def kernel(**inputs):
    import numpy as np
    import concourse.bacc as bacc
    from concourse.bass_utils import run_bass_kernel_spmd as run

    nc = bacc.Bacc("TRN2", target_bir_lowering=False, num_devices=1)
    arrays, args = {}, []
    for name in _INS:
        a = np.ascontiguousarray(inputs[name])
        arrays[f"in_{name}"] = a
        args.append(nc.dram_tensor(f"in_{name}", a.shape, mybir.dt.from_np(a.dtype), kind="ExternalInput").ap())
    out = nc.dram_tensor("out_0", inputs["x"].shape, F32, kind="ExternalOutput").ap()
    gnn_kernel(nc, *args, out)
    return run(nc, [arrays], core_ids=[0]).results[0]["out_0"]
```

```python
from contextlib import ExitStack

import concourse.bass as bass
from concourse import mybir

P = 128
F32 = mybir.dt.float32
BF16 = mybir.dt.bfloat16
I32 = mybir.dt.int32
ALU = mybir.AluOpType
ACT = mybir.ActivationFunctionType
AX = mybir.AxisListType
EPS = 1e-5

D = 128
TILE = 128
TPC = 4
CHUNK = TILE * TPC
CPG = 4
TPG = TPC * CPG
GROUP = CHUNK * CPG
TNODES = 128
TNODES_BITS = 7
WIN = 80
WPB = 4
NK = P // TPC
SPAN = 1 << 13


def take(eng, sem, n=1):
    eng.wait_ge(sem, n)
    eng.sem_inc(sem, -n)


def flat(ap):
    return ap.rearrange("p a b -> p (a b)")


def over(ap, like, n):
    return ap.rearrange("p (o n) -> p o n", o=1).to_broadcast([P, like, n])


def each(ap, inner):
    p, n = ap.shape
    return ap.rearrange("p (n o) -> p n o", o=1).to_broadcast([p, n, inner])


def gnn_kernel(nc, x, src, dst, etype, norm, weight, w_comp, loop_w, h_bias,
               theta, phi, fc1, g0, b0, g1, b1, out):
    N = x.shape[0]
    E = src.shape[0]
    R, B = w_comp.shape
    NW = (N + TNODES - 1) // TNODES
    NXW = (N + WIN - 1) // WIN
    LASTN = N - (NW - 1) * TNODES
    NBU = (NW + WPB - 1) // WPB
    NWP = NBU * WPB
    NG = (E + GROUP - 1) // GROUP
    NCH = NG * CPG
    NB = (NG * TPG + P - 1) // P
    FULLB = E // (P * TILE)
    LROWS = E // TILE - FULLB * P
    LEDGE = E % TILE
    LASTC = E - (NCH - 1) * CHUNK
    RW = R * D
    EB = NB * TILE
    EVEN, ODD = NG - NG // 2, NG // 2
    assert NG % 2 == 1 and NBU % 2 == 1 and NW % 2 == 1
    assert 0 < LASTC <= CHUNK and FULLB == NB - 1 and LEDGE and NW > (NBU - 1) * WPB

    ctx = ExitStack()

    def sb(name, shape, dt=F32):
        return ctx.enter_context(nc.sbuf_tensor(name, shape, dt))

    def sem(name):
        return ctx.enter_context(nc.semaphore(name))

    with ctx:
        table = nc.dram_tensor("table", [NW * TNODES * R, D], F32, kind="Internal").ap()
        wrel_d = nc.dram_tensor("wrel_d", [R, D * D], F32, kind="Internal").ap()
        atab = nc.dram_tensor("atab", [NWP * TNODES, 3 * D], BF16, kind="Internal").ap()
        btab = nc.dram_tensor("btab", [NWP * TNODES, D], F32, kind="Internal").ap()
        digits_d = nc.dram_tensor("digits_d", [2, NB * P * TILE], BF16, kind="Internal").ap()
        bounds_d = nc.dram_tensor("bounds_d", [NB, NK], I32, kind="Internal").ap()
        spill = nc.dram_tensor("spill", [NG, P, GROUP], F32, kind="Internal").ap()

        X = sb("X", [P, NWP, D])
        ACC = sb("ACC", [P, NWP * TNODES])
        iota_w = sb("iota_w", [P, TNODES])
        win_off = sb("win_off", [P, NXW + 1])
        node_col = sb("node_col", [P, NXW + 1])
        iota_h = sb("iota_h", [P, NW])
        ident = sb("ident", [P, P])
        ones = sb("ones", [P, P])
        onesb = sb("onesb", [P, P], BF16)
        idx0T = sb("idx0T", [P, NB * P], I32)
        srcT = sb("srcT", [P, NB * P], I32)
        dstT = sb("dstT", [P, NB * P])
        normT = sb("normT", [P, NB * P])
        hiT = sb("hiT", [P, NB * P])
        loT = sb("loT", [P, NB * P])
        bounds = sb("bounds", [1, NB * NK], I32)
        ix = sb("ix", [P, 2, TPG], I32)
        G = sb("G", [P, 2, TPG, D])
        oh = sb("oh", [P, 2, TPC, WIN])
        ohx = sb("ohx", [P, TPC, WIN])
        ohT = sb("ohT", [P, 2, CHUNK], BF16)
        ohTx = sb("ohTx", [P, CHUNK], BF16)
        oh_lo = sb("oh_lo", [P, 2, TPC, TNODES], BF16)
        oh_hi = sb("oh_hi", [P, 2, TPC, NW], BF16)
        small = sb("small", [P, 64])
        theta_s = sb("theta_s", [P, D])
        phi_s = sb("phi_s", [P, D])
        fc1_s = sb("fc1_s", [P, D])
        thph = sb("thph", [P, 2 * D])
        fc1T = sb("fc1T", [P, D])
        fc1sT = sb("fc1sT", [P, D])
        shift3 = sb("shift3", [96, TPC, D], BF16)
        diag = sb("diag", [P, D])
        diag_t = sb("diag_t", [P, D])
        loop_s = sb("loop_s", [P, D])
        bn_in = sb("bn_in", [P, 5])
        stats = sb("stats", [P, NCH, 6])
        ln_st = sb("ln_st", [P, NWP, 6])
        ln_mv = sb("ln_mv", [P, NWP, 2])
        ln_r = sb("ln_r", [P, NWP])
        rcnt = sb("rcnt", [P, NWP])
        xn = sb("xn", [P, 2, WPB * D])
        xT = sb("xT", [P, 2, WPB * D])
        bst = sb("bst", [P, 2, WPB * D])
        resid = sb("resid", [P, WPB * D])
        BIG = sb("BIG", [P, 3 * RW])
        tout = BIG[:, 0:2 * RW].rearrange("p (s n) -> p s n", s=2)
        wrel = BIG[:, 2 * RW:3 * RW]
        wst = tout[0:B, 0, :].rearrange("p (s n) -> p s n", s=2)
        ost = tout[0:R, 1, :].rearrange("p (s n) -> p s n", s=2)
        at = [0]

        def part(n):
            at[0] += n
            assert at[0] <= 3 * RW
            return BIG[:, at[0] - n:at[0]]
        stage = part(2 * GROUP).rearrange("p (s n) -> p s n", s=2)
        R2 = part(CPG * CHUNK).rearrange("p (s q d) -> p s q d", s=CPG, q=TPC)
        oh3 = part(GROUP)
        digits = oh3[0:2, :].bitcast(BF16).rearrange("p (s n) -> p s n", s=2)
        oh3 = oh3[:, 0:CPG * TPC * WIN].rearrange("p (s q n) -> p s q n", s=CPG, q=TPC)
        ast = part(WPB * 3 * D).bitcast(BF16).rearrange("p (s w a d) -> p s w a d", s=2, w=WPB, a=3)
        aw = part(CPG * 3 * D // 2).bitcast(BF16).rearrange("p (s a d) -> p s a d", s=CPG, a=3)
        dst_g = part(2 * TPG).rearrange("p (s t) -> p s t", s=2)
        awx = part(3 * D // 2).bitcast(BF16).rearrange("p (a d) -> p a d", a=3)
        hot = G[:, :, :, :].rearrange("p s t d -> p s (t d)")

        accf = ACC[:, :]
        gf = G[:, :, :, :].rearrange("p s t d -> p (s t d)")

        def rows(of, k, dt=F32):
            v = of[:, EB * k:EB * (k + 1)]
            return (v if dt is F32 else v.bitcast(dt)).rearrange("p (b e) -> p b e", b=NB)
        r_src, r_typ, r_dst = (rows(accf, k, I32) for k in range(3))
        r_nrm, f_idx, f_src, f_rel = (rows(accf, k) for k in range(3, 7))
        f_hi, f_lo, f_dst = (rows(gf, k) for k in range(3))
        a_hi = rows(gf, 3, I32)
        f_min = rows(wrel, 0)
        i_rel = rows(wrel, 1, I32)
        i_hi = rows(wrel, 2, I32)
        dig_hi, dig_lo = (wrel[:, 3 * EB + k * EB // 2:3 * EB + (k + 1) * EB // 2].bitcast(BF16)
                          .rearrange("p (b e) -> p b e", b=NB) for k in range(2))
        t_min = wrel[:, 4 * EB:4 * EB + NB]
        t_max = wrel[:, 4 * EB + NB:4 * EB + 2 * NB]
        t_base = wrel[:, 4 * EB + 2 * NB:4 * EB + 3 * NB]
        c_min = wrel[0:NB, 4 * EB + 32:4 * EB + 32 + NK]
        c_max = wrel[0:NB, 4 * EB + 64:4 * EB + 64 + NK]
        c_ext = wrel[0:NB, 4 * EB + 96:4 * EB + 96 + 2 * NK].bitcast(I32)
        c_win = wrel[0:NB, 4 * EB + 160:4 * EB + 160 + NK].bitcast(I32)
        c_tile = wrel[0:NB, 4 * EB + 224:4 * EB + 224 + P]

        PS = ctx.enter_context(nc.psum_tensor("PS", [P, 8, 512], F32))

        const_done = sem("const_done")
        pads_set = sem("pads_set")
        x_in = sem("x_in")
        edges_in = sem("edges_in")
        wts_in = sem("wts_in")
        wcomp_in = sem("wcomp_in")
        wst_in = [sem("wst_in0"), sem("wst_in1")]
        wst_used = sem("wst_used")
        ost_ready = sem("ost_ready")
        ost_out = [sem("ost_out0"), sem("ost_out1")]
        wrel_ps_free = sem("wrel_ps_free")
        wrel_in = sem("wrel_in")
        dve_self = sem("dve_self")
        act_self = sem("act_self")
        pool_self = sem("pool_self")
        rows_f = sem("rows_f")
        rows_f2 = sem("rows_f2")
        setup_out = sem("setup_out")
        rows_out = sem("rows_out")
        minmax = sem("minmax")
        minmax_T = sem("minmax_T")
        base_rows = sem("base_rows")
        base_T = sem("base_T")
        bnd_in = sem("bnd_in")
        rows_T = sem("rows_T")
        rows_T2 = sem("rows_T2")
        cols_ready = sem("cols_ready")
        wT_ps = sem("wT_ps")
        wT_done = sem("wT_done")
        xwin_ready = sem("xwin_ready")
        xwT_ps = sem("xwT_ps")
        xwT_ready = sem("xwT_ready")
        tab_ps_act = sem("tab_ps_act")
        tab_ps_dve = sem("tab_ps_dve")
        tab_free_act = sem("tab_free_act")
        tab_free_dve = sem("tab_free_dve")
        loop_ps = sem("loop_ps")
        loop_done = sem("loop_done")
        tout_act = sem("tout_act")
        tout_dve = sem("tout_dve")
        tout_out = [sem("tout_out0"), sem("tout_out1")]
        tout_free_act = sem("tout_free_act")
        tout_free_dve = sem("tout_free_dve")
        table_done = sem("table_done")
        ix_ready = sem("ix_ready")
        ix_free = sem("ix_free")
        gathered = [sem(f"gathered{i}") for i in range(2 * CPG)]
        g_free = sem("g_free")
        oh_ready = sem("oh_ready")
        oh_free = sem("oh_free")
        seg_ready = sem("seg_ready")
        seg_free = sem("seg_free")
        ohx_ready = sem("ohx_ready")
        segx_ready = sem("segx_ready")
        added = sem("added")
        cnt_oh = sem("cnt_oh")
        cnt_done = sem("cnt_done")
        ticks = {e: sem(f"tick_{e}") for e in ("pe", "act", "sp", "pool", "dve")}
        accw_ready = sem("accw_ready")
        accw_ps = sem("accw_ps")
        sums_turned = sem("sums_turned")
        accw_used = sem("accw_used")
        var_ready = sem("var_ready")
        sd_ready = sem("sd_ready")
        xn_ready = sem("xn_ready")
        xn_kept = sem("xn_kept")
        xn_free = sem("xn_free")
        nT_ps = sem("nT_ps")
        nT_ready = sem("nT_ready")
        a_ps = sem("a_ps")
        b_ps = sem("b_ps")
        b_copied = sem("b_copied")
        a_split = sem("a_split")
        ast_ready = sem("ast_ready")
        bst_ready = sem("bst_ready")
        ast_out = [sem("ast_out0"), sem("ast_out1")]
        bst_out = [sem("bst_out0"), sem("bst_out1")]
        tabs_done = sem("tabs_done")
        dig_in = [sem("dig_in0"), sem("dig_in1")]
        dig_free = sem("dig_free")
        aw_in = [sem(f"aw_in{k}") for k in range(CPG)]
        aw_free = sem("aw_free")
        awx_in = sem("awx_in")
        awx_free = sem("awx_free")
        d_ready = sem("d_ready")
        d_free = sem("d_free")
        ohT_ready = sem("ohT_ready")
        look_done = sem("look_done")
        ohTx_ready = sem("ohTx_ready")
        lookx_done = sem("lookx_done")
        e_ready = sem("e_ready")
        e_free = sem("e_free")
        e_copied = sem("e_copied")
        e_measured = sem("e_measured")
        stored = [sem("stored0"), sem("stored1")]
        bn0_ready = sem("bn0_ready")
        st_in = [sem("st_in0"), sem("st_in1")]
        st_free = sem("st_free")
        hot_ready = sem("hot_ready")
        hot_free = sem("hot_free")
        e2_ready = sem("e2_ready")
        e2_free = sem("e2_free")
        bn_var = sem("bn_var")
        bn_sd = sem("bn_sd")
        fc1_scaled = sem("fc1_scaled")
        fc1s_ps = sem("fc1s_ps")
        pass3_go = sem("pass3_go")
        y_ready = sem("y_ready")
        r2_ready = sem("r2_ready")
        r2_free = sem("r2_free")
        res_ready = sem("res_ready")
        res_out = [sem("res_out0"), sem("res_out1")]

        def reached(eng, name, s, value):
            eng.wait_ge(s, value)
            eng.sem_inc(ticks[name], 1)

        def by_pairs(eng, n, body):
            body(0, 0, 0)
            body(1, 1, 0)
            with eng.Fori(1, n // 2) as i:
                body(2 * i, 0, i)
                body(2 * i + 1, 1, i)
            body(n - 1, 0, n // 2)

        def first_use(use):
            return isinstance(use, int) and use == 0

        def last(i, n):
            return isinstance(i, int) and i == n - 1

        def after(g, h, use, k):
            if k + 1 < CPG:
                return g, h, use, k + 1
            if last(g, NG):
                return None
            return g + 1, 1 - h, use + h, 0

        def reach_of(eng, c):
            return eng.value_load(bounds[0:1, bass.ds(c, 1)], min_val=SPAN, max_val=SPAN * (NXW + 1) - 1)

        def least_dst(eng, reach):
            return nc.s_assert_within(reach % SPAN, 0, N - 1, skip_runtime_bounds_check_because="it is a node")

        def further_windows(eng, reach, body):
            with eng.If(reach >= 2 * SPAN):
                with eng.Fori(1, reach // SPAN) as i:
                    body(i)

        def win(t, w):
            return t[:, bass.ds(w, 1), :].rearrange("p o d -> p (o d)")

        block = ctx.enter_context(nc.Block())

        @block.sync
        def _(sp):
            sp.wait_ge(pads_set, 5)
            norm_v = norm.rearrange("e o -> (e o)")
            at_e = FULLB * P * TILE
            for vec, r in ((dst, r_dst), (src, r_src), (etype, r_typ), (norm_v, r_nrm)):
                sp.dma_start(r[:, 0:FULLB, :], vec[0:at_e].rearrange("(b p e) -> p b e", p=P, e=TILE)).then_inc(edges_in, 16)
                sp.dma_start(r[0:LROWS, FULLB, :],
                             vec[at_e:at_e + LROWS * TILE].rearrange("(p e) -> p e", e=TILE)).then_inc(edges_in, 16)
                sp.dma_start(r[LROWS:LROWS + 1, FULLB, 0:LEDGE],
                             vec[E - LEDGE:E].rearrange("(p e) -> p e", p=1)).then_inc(edges_in, 16)
            wv = weight.rearrange("b d f -> b (d f)")
            n = RW // 2
            pieces = D * D // n
            sp.dma_start(small[0:B, 0:R], w_comp.rearrange("r b -> b r"),
                         allow_slow_non_contiguous=True).then_inc(wcomp_in, 16)
            for s in range(pieces + 1):
                if s < pieces:
                    if s >= 2:
                        sp.wait_ge(wst_used, 4 * (s - 1))
                    sp.dma_start(wst[:, s % 2, :], wv[:, s * n:(s + 1) * n]).then_inc(wst_in[s % 2], 16)
                if s >= 1:
                    take(sp, ost_ready)
                    sp.dma_start(wrel_d[:, (s - 1) * n:s * n], ost[:, (s - 1) % 2, :]).then_inc(ost_out[(s - 1) % 2], 16)
            for a, t in ((loop_s, loop_w), (theta_s, theta), (phi_s, phi), (fc1_s, fc1)):
                sp.dma_start(a[:, :], t).then_inc(wts_in, 16)
            for k, v in enumerate((g0, b0, g1, b1, h_bias)):
                sp.dma_start(bn_in[:, k:k + 1], v.rearrange("(f o) -> f o", o=1)).then_inc(wts_in, 16)
            sp.dma_start(X[:, 0:NW - 1, :], x[0:(NW - 1) * TNODES, :].rearrange("(w p) d -> p w d", p=P)).then_inc(x_in, 16)
            sp.dma_start(X[0:LASTN, NW - 1, :], x[(NW - 1) * TNODES:N, :]).then_inc(x_in, 16)
            sp.wait_ge(setup_out, 2)
            for k, dg in enumerate((dig_hi, dig_lo)):
                sp.dma_start(digits_d[k, :].rearrange("(b p e) -> p b e", p=P, e=TILE), dg).then_inc(rows_out, 16)
            sp.dma_start(bounds_d[:, :], c_win).then_inc(rows_out, 16)
            sp.wait_ge(rows_out, 48)
            sp.dma_start(bounds[:, :], bounds_d.rearrange("(o b) c -> o (b c)", o=1)).then_inc(bnd_in, 16)
            for q in range(2):
                sp.wait_ge(ost_out[q], 16 * pieces // 2)
            sp.dma_start(wrel.rearrange("p (r f) -> p r f", r=R),
                         wrel_d.rearrange("r (d f) -> d r f", d=D)).then_inc(wrel_in, 16)

            def store_table(w, s, use):
                take(sp, tout_act)
                take(sp, tout_dve)
                sp.dma_start(table[bass.ds(w * (TNODES * R), TNODES * R), :].rearrange("(p r) d -> p (r d)", p=P),
                             tout[:, s, :]).then_inc(tout_out[s], 16)
                if s == 1 or not first_use(use):
                    reached(sp, "sp", tout_out[1 - s], 16 * (use + s))
                    sp.sem_inc(tout_free_act, 1)
                    sp.sem_inc(tout_free_dve, 1)
            by_pairs(sp, NW, store_table)
            sp.wait_ge(tout_out[0], 16 * (NW - NW // 2))
            sp.wait_ge(tout_out[1], 16 * (NW // 2))
            sp.sem_inc(table_done, 1)

            def store_tables(u, s, use):
                rows_u = bass.ds(u * (WPB * TNODES), WPB * TNODES)
                take(sp, bst_ready)
                sp.dma_start(btab[rows_u, :].rearrange("(w p) d -> p w d", p=P),
                             bst[:, s, :].rearrange("p (w d) -> p w d", w=WPB)).then_inc(bst_out[s], 16)
                take(sp, ast_ready)
                sp.dma_start(atab[rows_u, :].rearrange("(w p) n -> p w n", p=P),
                             ast[:, s, :, :, :].rearrange("p w a d -> p w (a d)")).then_inc(ast_out[s], 16)
            by_pairs(sp, NBU, store_tables)
            for o in (ast_out, bst_out):
                sp.wait_ge(o[0], 16 * (NBU - NBU // 2))
                sp.wait_ge(o[1], 16 * (NBU // 2))
            sp.sem_inc(tabs_done, 1)

            def load_digits(g, h):
                take(sp, dig_free)
                sp.dma_start(digits[:, h, :], digits_d[:, bass.ds(g * GROUP, GROUP)]).then_inc(dig_in[h], 16)

            def load_windows(g, h, use):
                for k in range(CPG):
                    if k == CPG // 2 and not last(g, NG):
                        load_digits(g + 1, 1 - h)
                    reach = reach_of(sp, CPG * g + k)
                    base = least_dst(sp, reach)
                    take(sp, aw_free)
                    sp.dma_start(aw[0:WIN, k, :, :].rearrange("p a d -> p (a d)"), atab[bass.ds(base, WIN), :]).then_inc(aw_in[k], 16)

                    def further(i):
                        take(sp, awx_free)
                        at_w = nc.s_assert_within(base + i * WIN, 0, N - 1, skip_runtime_bounds_check_because="no window starts past the greatest dst")
                        sp.dma_start(awx[0:WIN].rearrange("p a d -> p (a d)"), atab[bass.ds(at_w, WIN), :]).then_inc(awx_in, 16)
                    further_windows(sp, reach, further)
            load_digits(0, 0)
            by_pairs(sp, NG, load_windows)

            sp.wait_ge(stored[0], 16 * EVEN)
            sp.wait_ge(stored[1], 16 * ODD)

            def load_e(g, h, use):
                take(sp, st_free)
                sp.dma_start(stage[:, h, :], spill[bass.ds(g, 1), :, :].rearrange("o p n -> (o p) n")).then_inc(st_in[h], 16)
            for _ in range(2):
                take(sp, st_free, 2)
                sp.sem_inc(st_free, 2)
                by_pairs(sp, NG, load_e)

            def store_out(u, s, use):
                take(sp, res_ready)
                r = xn[:, s, :].rearrange("p (w d) -> p w d", w=WPB)
                if last(u, NBU):
                    full = NW - 1 - WPB * u
                    if full:
                        sp.dma_start(out[u * WPB * TNODES:(NW - 1) * TNODES, :].rearrange("(w p) d -> p w d", p=P),
                                     r[:, 0:full, :]).then_inc(res_out[s], 16)
                    sp.dma_start(out[(NW - 1) * TNODES:N, :], r[0:LASTN, full, :]).then_inc(res_out[s], 16)
                    sp.wait_ge(res_out[s], 16 * (use + 1 + (full > 0)))
                else:
                    sp.dma_start(out[bass.ds(u * (WPB * TNODES), WPB * TNODES), :].rearrange("(w p) d -> p w d", p=P), r)\
                      .then_inc(res_out[s], 16)
            by_pairs(sp, NBU, store_out)
            sp.wait_ge(res_out[1], 16 * (NBU // 2))

        @block.gpsimd
        def _(pool):
            nc.gpsimd.memset(r_dst[:, FULLB, :], -1).then_inc(pads_set, 1)
            nc.gpsimd.memset(r_src[:, FULLB, :], 0).then_inc(pads_set, 1)
            nc.gpsimd.memset(r_typ[:, FULLB, :], 0).then_inc(pads_set, 1)
            nc.gpsimd.memset(X[:, NW - 1:NWP, :], 0.0).then_inc(pads_set, 1)
            nc.gpsimd.memset(r_nrm[:, FULLB, :], 0.0).then_inc(pads_set, 1)
            nc.gpsimd.memset(ones[:, :], 1.0).then_inc(const_done, 1)
            nc.gpsimd.memset(onesb[:, :], 1.0).then_inc(const_done, 1)
            nc.gpsimd.memset(ident[:, :], 0.0).then_inc(const_done, 1)
            pool.wait_ge(const_done, 3)
            nc.gpsimd.affine_select(out=ident[:, :], in_=ident[:, :], compare_op=ALU.not_equal, fill=1.0, base=0,
                                    pattern=[[-1, P]], channel_multiplier=1).then_inc(const_done, 1)
            for t, step, n, cm in ((iota_w, 1, TNODES, 0), (win_off, WIN, NXW + 1, 0), (node_col, WIN, NXW + 1, 1), (iota_h, 1, NW, 0)):
                nc.gpsimd.iota(t[:, :], pattern=[[step, n]], base=0, channel_multiplier=cm,
                               allow_small_or_imprecise_dtypes=True).then_inc(const_done, 1)
            pool.sem_inc(g_free, 2 * CPG)
            pool.sem_inc(ix_free, 2)

            def gathers(rows_of):
                def one(g, h, use):
                    take(pool, ix_ready)
                    for k in range(CPG):
                        take(pool, g_free)
                        for q in range(TPC):
                            t = TPC * k + q
                            nc.gpsimd.indirect_dma_start(
                                out=G[:, h, t, :], out_offset=None, in_=rows_of,
                                in_offset=bass.IndirectOffsetOnAxis(ap=ix[:, h, t:t + 1], axis=0),
                            ).then_inc(gathered[CPG * h + k], 16)
                by_pairs(pool, NG, one)

            pool.wait_ge(table_done, 1)
            gathers(table[:, :])

            def keep(u, s, use):
                take(pool, xn_kept)
                nc.gpsimd.tensor_copy(flat(X[:, bass.ds(u * WPB, WPB), :]), xn[:, s, :]).then_inc(xn_free, 1)
            by_pairs(pool, NBU, keep)

            pool.wait_ge(tabs_done, 1)
            gathers(btab[:, :])

            pool.wait_ge(pass3_go, 1)

            def one_hots(g, h, use):
                nc.gpsimd.tensor_copy(dst_g[:, h, :], dstT[:, bass.ds(TPG * g, TPG)]).then_inc(pool_self, 1)
                take(pool, pool_self)
                for k in range(CPG):
                    take(pool, oh_free)
                    for q in range(TPC):
                        t = TPC * k + q
                        ins = nc.gpsimd.tensor_scalar(oh3[:, k, q, :], iota_w[:, 0:WIN], dst_g[:, h, t:t + 1], None, ALU.is_equal)
                    ins.then_inc(oh_ready, 1)
            by_pairs(pool, NG, one_hots)

        @block.tensor
        def _(pe):
            pe.wait_ge(const_done, 8)
            pe.wait_ge(minmax, 2)
            pe.transpose(PS[0:NB, 0, 0:P], t_min, ident[:, :])
            pe.transpose(PS[0:NB, 0, P:2 * P], t_max, ident[:, :]).then_inc(minmax_T, 1)
            take(pe, base_rows)
            pe.transpose(PS[:, 1, 0:NB], c_tile, ident[0:NB, 0:NB]).then_inc(base_T, 1)
            pe.wait_ge(wcomp_in, 16)
            pe.wait_ge(rows_f, 3)
            n = RW // 2
            for s in range(D * D // n):
                pe.wait_ge(wst_in[s % 2], 16 * (s // 2 + 1))
                if s >= 2:
                    take(pe, wrel_ps_free)
                for j in range(n // 512):
                    pe.matmul(PS[0:R, 4 * (s % 2) + j, :], small[0:B, 0:R], wst[:, s % 2, j * 512:(j + 1) * 512],
                              start=True, stop=True).then_inc(wst_used, 1)
            pe.wait_ge(wrel_ps_free, 2)
            for k, f in enumerate((f_idx, f_src, f_rel, r_nrm)):
                for b in range(NB):
                    mm = pe.transpose(PS[:, 2 * k + b // 4, (b % 4) * P:(b % 4 + 1) * P], f[:, b, :], ident[:, :])
                mm.then_inc(rows_T, 1)
            pe.wait_ge(rows_f2, 2)
            for k, f in enumerate((f_hi, f_lo)):
                pe.wait_ge(cols_ready, k + 1)
                for b in range(NB):
                    mm = pe.transpose(PS[:, 2 * k + b // 4, (b % 4) * P:(b % 4 + 1) * P], f[:, b, :], ident[:, :])
                mm.then_inc(rows_T2, 1)
            pe.wait_ge(wts_in, 16 * 9)
            pe.wait_ge(cols_ready, 4)
            for k, a in enumerate((theta_s, phi_s, fc1_s)):
                mm = pe.transpose(PS[:, 4, k * D:(k + 1) * D], a[:, :], ident[:, :])
            mm.then_inc(wT_ps, 1)
            pe.wait_ge(wT_done, 1)

            pe.wait_ge(wrel_in, 16)

            def turn_window(s):
                take(pe, xwin_ready)
                pe.transpose(PS[:, 0, 0:P], xn[:, s, 0:D], ident[:, :]).then_inc(xwT_ps, 1)

            def table_rows(w, s, use):
                take(pe, xwT_ready)
                for j in range(RW // 512):
                    if j == 2 and not last(w, NW):
                        turn_window(1 - s)
                    free, full = ((tab_free_act, tab_ps_act), (tab_free_dve, tab_ps_dve))[j % 2]
                    take(pe, free)
                    pe.matmul(PS[:, 2 + j % 2 + 2 * ((j // 2) % 2), :], xT[:, s, 0:D], wrel[:, j * 512:(j + 1) * 512],
                              start=True, stop=True).then_inc(full, 1)
                take(pe, loop_done)
                pe.matmul(PS[:, 1, 0:D], loop_s[:, :], xT[:, s, 0:D], start=True, stop=True).then_inc(loop_ps, 1)
            turn_window(0)
            by_pairs(pe, NW, table_rows)

            pe.wait_ge(bnd_in, 16)

            def add_messages(g, h, use):
                for k in range(CPG):
                    reached(pe, "pe", gathered[CPG * h + k], 16 * TPC * (use + 1))
                    take(pe, seg_free)
                    take(pe, oh_ready)
                    for q in range(TPC):
                        mm = pe.matmul(PS[:, k % 2, 0:WIN], G[:, h, TPC * k + q, :], oh[:, k % 2, q, :],
                                       start=(q == 0), stop=(q == TPC - 1))
                    mm.then_inc(seg_ready, 1)
                    take(pe, cnt_oh)
                    for q in range(TPC):
                        mm = pe.matmul(PS[:, 7, 0:NW], oh_lo[:, k % 2, q, :], oh_hi[:, k % 2, q, :],
                                       start=(isinstance(g, int) and g == 0 and k == 0 and q == 0),
                                       stop=(last(g, NG) and k == CPG - 1 and q == TPC - 1), skip_group_check=True)
                    mm.then_inc(cnt_done, 1)

                    def further(i):
                        take(pe, ohx_ready)
                        for q in range(TPC):
                            mm = pe.matmul(PS[:, 2, 0:WIN], G[:, h, TPC * k + q, :], ohx[:, q, :],
                                           start=(q == 0), stop=(q == TPC - 1))
                        mm.then_inc(segx_ready, 1)
                    further_windows(pe, reach_of(pe, CPG * g + k), further)
            by_pairs(pe, NG, add_messages)

            def turn_sums(u, s, use):
                take(pe, accw_ready)
                take(pe, accw_used)
                for w in range(WPB):
                    mm = pe.transpose(PS[:, s, w * D:(w + 1) * D], xT[:, s, w * D:(w + 1) * D], ident[:, :])
                mm.then_inc(sums_turned, 1)
            by_pairs(pe, NBU, turn_sums)

            def node_tables(u, s, use):
                take(pe, xn_ready)
                for w in range(WPB):
                    mm = pe.transpose(PS[:, 2 + s, w * D:(w + 1) * D], xn[:, s, w * D:(w + 1) * D], ident[:, :])
                mm.then_inc(nT_ps, 1)
                take(pe, nT_ready)
                for half, bank, free, full in ((0, 4 + s, a_split, a_ps), (1, 6 + s, b_copied, b_ps)):
                    take(pe, free)
                    for w in range(WPB):
                        mm = pe.matmul(PS[:, bank, w * D:(w + 1) * D], xT[:, s, w * D:(w + 1) * D],
                                       thph[:, half * D:(half + 1) * D], start=(w == 0), stop=(w == WPB - 1), skip_group_check=True)
                    mm.then_inc(full, 1)
            by_pairs(pe, NBU, node_tables)

            def spread_dst(g, h, use, k):
                if k == 0:
                    reached(pe, "pe", dig_in[h], 16 * (use + 1))
                take(pe, d_free)
                pe.matmul(PS[:, k % 2, :], onesb[0:2, :], digits[:, h, k * CHUNK:(k + 1) * CHUNK],
                          start=True, stop=True).then_inc(d_ready, 1)

            def edge_features(g, h, use):
                for k in range(CPG):
                    reach = reach_of(pe, CPG * g + k)
                    reached(pe, "pe", gathered[CPG * h + k], 16 * TPC * (use + 1 + (EVEN, ODD)[h]))
                    take(pe, e_free)
                    for q in range(TPC):
                        pe.matmul(PS[:, 2 + k % 2, q * TILE:(q + 1) * TILE], G[:, h, TPC * k + q, :], ident[:, :],
                                  start=(q == 0), stop=False, skip_group_check=True)
                    nxt = after(g, h, use, k)
                    if nxt:
                        spread_dst(*nxt)
                    reached(pe, "pe", aw_in[k], 16 * (g + 1))
                    take(pe, ohT_ready)
                    for a in range(3):
                        mm = pe.matmul(PS[:, 2 + k % 2, :], aw[0:WIN, k, a, :], ohT[0:WIN, k % 2, :],
                                       start=False, stop=(a == 2), skip_group_check=True)
                    mm.then_inc(look_done, 1)

                    def further(i):
                        take(pe, awx_in, 16)
                        take(pe, ohTx_ready)
                        for a in range(3):
                            mm = pe.matmul(PS[:, 2 + k % 2, :], awx[0:WIN, a, :], ohTx[0:WIN, :],
                                           start=False, stop=(a == 2), skip_group_check=True)
                        mm.then_inc(lookx_done, 1)
                    further_windows(pe, reach, further)
            spread_dst(0, 0, 0, 0)
            by_pairs(pe, NG, edge_features)

            def second_product(g, h, use):
                take(pe, hot_ready)
                pe.sem_inc(st_free, 1)
                for k in range(CPG):
                    take(pe, e2_free)
                    pe.matmul(PS[:, CPG * h + k, :], fc1T[:, :], hot[:, h, k * CHUNK:(k + 1) * CHUNK],
                              start=True, stop=True).then_inc(e2_ready, 1)
            by_pairs(pe, NG, second_product)

            take(pe, fc1_scaled)
            pe.transpose(PS[:, 0, 0:D], diag[:, :], ident[:, :])
            pe.matmul(PS[:, 1, 0:D], ones[:, :], diag_t[:, :], start=True, stop=True).then_inc(fc1s_ps, 1)
            pe.wait_ge(pass3_go, 1)

            def second_again(g, h, use, k):
                take(pe, hot_ready)
                if k == CPG - 1:
                    pe.sem_inc(st_free, 1)
                pe.matmul(PS[:, k, :], onesb[0:96, :], shift3[:, :, :].rearrange("p q d -> p (q d)"),
                          start=True, stop=False, skip_group_check=True)
                for q in range(TPC):
                    t = TPC * k + q
                    mm = pe.matmul(PS[:, k, q * D:(q + 1) * D], hot[:, h, t * TILE:(t + 1) * TILE], fc1sT[:, :],
                                   start=False, stop=(q == TPC - 1), skip_group_check=True)
                mm.then_inc(y_ready, 1)

            def sum_edges(g, h, use):
                for k in range(CPG):
                    nxt = (g, h, use, k)
                    for _ in range(3):
                        nxt = nxt and after(*nxt)
                    if nxt:
                        second_again(*nxt)
                    take(pe, r2_ready)
                    take(pe, seg_free)
                    take(pe, oh_ready)
                    for q in range(TPC):
                        mm = pe.matmul(PS[:, 4 + k % 2, 0:WIN], R2[:, k, q, :], oh3[:, k, q, :],
                                       start=(q == 0), stop=(q == TPC - 1))
                    mm.then_inc(seg_ready, 1)

                    def further(i):
                        take(pe, ohx_ready)
                        for q in range(TPC):
                            mm = pe.matmul(PS[:, 6, 0:WIN], R2[:, k, q, :], ohx[:, q, :],
                                           start=(q == 0), stop=(q == TPC - 1))
                        mm.then_inc(segx_ready, 1)
                    further_windows(pe, reach_of(pe, CPG * g + k), further)
            second_again(0, 0, 0, 0)
            second_again(0, 0, 0, 1)
            second_again(0, 0, 0, 2)
            by_pairs(pe, NG, sum_edges)
            by_pairs(pe, NBU, turn_sums)

        @block.scalar
        def _(act):
            act.wait_ge(const_done, 8)
            n = RW // 2
            for s in range(D * D // n):
                act.wait_ge(wst_used, 4 * (s + 1))
                if s >= 2:
                    act.wait_ge(ost_out[s % 2], 16 * (s // 2))
                act.activation(ost[:, s % 2, :], PS[0:R, 4 * (s % 2):4 * (s % 2) + 4, :].rearrange("p b n -> p (b n)"),
                               ACT.Copy).then_inc(act_self, 1)
                take(act, act_self)
                act.sem_inc(wrel_ps_free, 1)
                act.sem_inc(ost_ready, 1)
            act.sem_inc(tab_free_act, 2)

            def copy_turned(s):
                take(act, xwT_ps)
                act.activation(xT[:, s, 0:D], PS[:, 0, 0:P], ACT.Copy).then_inc(xwT_ready, 1)

            def table_half(w, s, use):
                take(act, tout_free_act)
                for j in range(0, RW // 512, 2):
                    if j == 4 and not last(w, NW):
                        copy_turned(1 - s)
                    take(act, tab_ps_act)
                    act.activation(tout[:, s, j * 512:(j + 1) * 512], PS[:, 2 + 2 * ((j // 2) % 2), :],
                                   ACT.Copy).then_inc(tab_free_act, 1)
                act.drain().then_inc(tout_act, 1)
            act.wait_ge(wT_done, 1)
            copy_turned(0)
            by_pairs(act, NW, table_half)

            act.wait_ge(cols_ready, 4)

            def indices(g, h, use):
                take(act, ix_free)
                act.activation(ix[:, h, :], idx0T[:, bass.ds(g * TPG, TPG)], ACT.Copy).then_inc(ix_ready, 1)
            by_pairs(act, NG, indices)

            def copy_sums(u, s, use):
                if not first_use(use):
                    take(act, accw_ps)
                act.activation(xT[:, s, :], ACC[:, bass.ds(u * (WPB * TNODES), WPB * TNODES)], ACT.Copy).then_inc(accw_ready, 1)

            def turned_sums():
                by_pairs(act, NBU, copy_sums)
                take(act, accw_ps, 2)

            turned_sums()
            take(act, var_ready)
            act.activation(ln_r[:, :], ln_mv[:, :, 1], ACT.Sqrt).then_inc(sd_ready, 1)

            def copy_b(u, s, use):
                take(act, nT_ps)
                act.activation(xT[:, s, :], PS[:, 2 + s, :], ACT.Copy).then_inc(nT_ready, 1)
                take(act, b_ps)
                if not first_use(use):
                    reached(act, "act", bst_out[s], 16 * use)
                act.activation(bst[:, s, :], PS[:, 6 + s, :], ACT.Copy).then_inc(act_self, 1)
                take(act, act_self)
                act.sem_inc(bst_ready, 1)
                act.sem_inc(b_copied, 1)
            act.sem_inc(b_copied, 2)
            by_pairs(act, NBU, copy_b)

            for h in range(2):
                take(act, ix_free)
                act.activation(ix[:, h, :], srcT[:, h * TPG:(h + 1) * TPG], ACT.Copy).then_inc(ix_ready, 1)
            act.sem_inc(e_free, 2)

            def store_e(g, h, use):
                if not first_use(use):
                    reached(act, "act", stored[h], 16 * use)
                    take(act, e_measured)
                for k in range(CPG):
                    take(act, e_ready)
                    act.activation(stage[:, h, k * CHUNK:(k + 1) * CHUNK], PS[:, 2 + k % 2, :],
                                   ACT.Copy).then_inc(act_self, 1)
                    take(act, act_self)
                    act.sem_inc(e_free, 1)
                    act.sem_inc(e_copied, 1)
                act.dma_start(spill[bass.ds(g, 1), :, :].rearrange("o p n -> (o p) n"), stage[:, h, :]).then_inc(stored[h], 16)
                if not isinstance(g, int) or g + 2 < NG:
                    take(act, ix_free)
                    act.activation(ix[:, h, :], srcT[:, bass.ds((g + 2) * TPG, TPG)], ACT.Copy).then_inc(ix_ready, 1)
            store_e(0, 0, 0)
            store_e(1, 1, 0)
            with act.Fori(1, NG // 2 - 1) as i:
                store_e(2 * i, 0, i)
                store_e(2 * i + 1, 1, i)
            for g in range(NG - 3, NG):
                store_e(g, g % 2, g // 2)
            take(act, e_measured, 2)
            act.sem_inc(st_free, 2)
            act.sem_inc(hot_free, 2)

            def deviation(at):
                take(act, bn_var)
                act.activation(small[:, at + 3:at + 4], small[:, at + 2:at + 3], ACT.Sqrt).then_inc(bn_sd, 1)
            deviation(0)
            act.wait_ge(bn0_ready, 1)

            def relu_e(g, h, use):
                reached(act, "act", st_in[h], 16 * (use + 1))
                take(act, hot_free)
                act.activation(hot[:, h, :], stage[:, h, :], ACT.Relu, bias=small[:, 6:7],
                               scale=small[:, 5:6]).then_inc(hot_ready, 1)
            by_pairs(act, NG, relu_e)
            deviation(8)
            act.wait_ge(pass3_go, 1)

            def relu_e_again(g, h, use, k):
                if k == 0:
                    reached(act, "act", st_in[h], 16 * (use + 1 + (EVEN, ODD)[h]))
                c = slice(k * CHUNK, (k + 1) * CHUNK)
                act.activation(hot[:, h, c], stage[:, h, c], ACT.Relu, bias=small[:, 6:7],
                               scale=small[:, 5:6]).then_inc(hot_ready, 1)

            def relu_e2(g, h, use):
                for k in range(CPG):
                    if not last(g, NG):
                        relu_e_again(g + 1, 1 - h, use + h, k)
                    take(act, y_ready)
                    take(act, r2_free)
                    act.activation(R2[:, k, :, :].rearrange("p q d -> p (q d)"), PS[:, k, :],
                                   ACT.Relu).then_inc(r2_ready, 1)
            for k in range(CPG):
                relu_e_again(0, 0, 0, k)
            by_pairs(act, NG, relu_e2)

            turned_sums()
            take(act, var_ready)
            act.activation(ln_r[:, :], ln_mv[:, :, 1], ACT.Sqrt).then_inc(sd_ready, 1)

        @block.vector
        def _(dve):
            def step(ins):
                ins.then_inc(dve_self, 1)
                take(dve, dve_self)

            dve.wait_ge(const_done, 8)
            dve.wait_ge(edges_in, 16 * 12)
            step(dve.tensor_copy(f_dst, r_dst))
            step(dve.tensor_scalar(f_min, f_dst, 0.0, float(1 << 13), ALU.is_lt, ALU.mult))
            step(dve.tensor_tensor(f_min, f_min, f_dst, ALU.add))
            dve.tensor_reduce(t_min, f_min, AX.X, ALU.min).then_inc(minmax, 1)
            dve.tensor_reduce(t_max, f_dst, AX.X, ALU.max).then_inc(minmax, 1)
            step(dve.scalar_tensor_tensor(out=f_idx, in0=r_src, scalar=float(R), in1=r_typ, op0=ALU.mult, op1=ALU.add))
            dve.sem_inc(rows_f, 1)
            step(dve.tensor_copy(f_src, r_src))
            dve.sem_inc(rows_f, 1)
            take(dve, minmax_T)
            dve.tensor_reduce(c_max, PS[0:NB, 0, P:2 * P].rearrange("b (c t) -> b c t", t=TPC), AX.X, ALU.max)
            step(dve.tensor_reduce(c_min, PS[0:NB, 0, 0:P].rearrange("b (c t) -> b c t", t=TPC), AX.X, ALU.min))
            step(dve.tensor_copy(c_tile.rearrange("b (c t) -> b c t", t=TPC), each(c_min, TPC)))
            dve.sem_inc(base_rows, 1)
            step(dve.tensor_tensor(c_max, c_max, c_min, ALU.subtract))
            step(dve.tensor_copy(c_ext[:, 0:NK], c_max))
            assert WIN == 16 * 5 and N <= 16 * 1023
            step(dve.tensor_scalar(c_ext[:, NK:2 * NK], c_ext[:, 0:NK], 4, None, ALU.arith_shift_right))
            step(dve.tensor_scalar(c_ext[:, 0:NK], c_ext[:, NK:2 * NK], 205.0, None, ALU.mult))
            step(dve.tensor_scalar(c_ext[:, NK:2 * NK], c_ext[:, 0:NK], 10, None, ALU.arith_shift_right))
            step(dve.tensor_scalar(c_min, c_min, float(SPAN), None, ALU.add))
            step(dve.scalar_tensor_tensor(out=c_win, in0=c_ext[:, NK:2 * NK], scalar=float(SPAN), in1=c_min,
                                          op0=ALU.mult, op1=ALU.add))
            dve.sem_inc(setup_out, 1)
            take(dve, base_T)
            step(dve.tensor_copy(t_base, PS[:, 1, 0:NB]))
            step(dve.tensor_tensor(f_rel, f_dst, each(t_base, TILE), ALU.subtract))
            dve.sem_inc(rows_f, 1)
            step(dve.tensor_copy(i_rel, f_rel))
            step(dve.tensor_scalar(i_hi, i_rel, TNODES_BITS, None, ALU.arith_shift_right))
            dve.tensor_scalar(dig_hi, i_hi, float(TNODES), None, ALU.mult)
            step(dve.scalar_tensor_tensor(out=dig_lo, in0=i_hi, scalar=-float(TNODES), in1=i_rel, op0=ALU.mult, op1=ALU.add))
            dve.sem_inc(setup_out, 1)
            step(dve.tensor_scalar(a_hi, r_dst, TNODES_BITS, None, ALU.arith_shift_right))
            step(dve.tensor_copy(f_hi, a_hi))
            dve.sem_inc(rows_f2, 1)
            step(dve.scalar_tensor_tensor(out=f_lo, in0=f_hi, scalar=-float(TNODES), in1=f_dst, op0=ALU.mult, op1=ALU.add))
            dve.sem_inc(rows_f2, 1)
            for k, to in enumerate((idx0T, srcT, dstT, normT)):
                dve.wait_ge(rows_T, k + 1)
                dve.tensor_copy(to[:, :], flat(PS[:, 2 * k:2 * k + 2, :])[:, 0:NB * P]).then_inc(cols_ready, 1)
            for k, to in enumerate((hiT, loT)):
                dve.wait_ge(rows_T2, k + 1)
                step(dve.tensor_copy(to[:, :], flat(PS[:, 2 * k:2 * k + 2, :])[:, 0:NB * P]))
            dve.wait_ge(wT_ps, 1)
            step(dve.tensor_copy(thph[:, 0:D], PS[:, 4, 0:D]))
            step(dve.tensor_copy(fc1T[:, :], PS[:, 4, 2 * D:3 * D]))
            step(dve.tensor_tensor(thph[:, D:2 * D], PS[:, 4, D:2 * D], thph[:, 0:D], ALU.subtract))
            step(dve.memset(ACC[:, NW * TNODES:NWP * TNODES], 0.0))
            dve.wait_ge(x_in, 32)
            dve.sem_inc(wT_done, 1)
            dve.sem_inc(tab_free_dve, 2)
            dve.sem_inc(tout_free_act, 2)
            dve.sem_inc(tout_free_dve, 2)
            dve.sem_inc(loop_done, 1)

            def fix_window(w, s):
                dve.tensor_copy(xn[:, s, 0:D], win(X, w)).then_inc(xwin_ready, 1)

            def table_half(w, s, use):
                take(dve, tout_free_dve)
                for j in range(1, RW // 512, 2):
                    if j == 1 and not last(w, NW):
                        fix_window(w + 1, 1 - s)
                    take(dve, tab_ps_dve)
                    dve.tensor_copy(tout[:, s, j * 512:(j + 1) * 512], PS[:, 3 + 2 * ((j // 2) % 2), :]).then_inc(tab_free_dve, 1)
                dve.drain().then_inc(tout_dve, 1)
                take(dve, loop_ps)
                dve.tensor_scalar(ACC[:, bass.ds(w * TNODES, TNODES)], PS[:, 1, 0:D], bn_in[:, 4:5], None, ALU.add).then_inc(loop_done, 1)
            fix_window(0, 0)
            by_pairs(dve, NW, table_half)

            dve.wait_ge(bnd_in, 16)

            def one_hots(g, k):
                for q in range(TPC):
                    t = TPG * g + TPC * k + q
                    ins = dve.tensor_scalar(oh[:, k % 2, q, :], iota_w[:, 0:WIN], dstT[:, bass.ds(t, 1)],
                                            normT[:, bass.ds(t, 1)], ALU.is_equal, ALU.mult)
                ins.then_inc(oh_ready, 1)

            def add_sums(g, k, bank, scaled):
                reach = reach_of(dve, CPG * g + k)
                base = least_dst(dve, reach)
                acc = ACC[:, bass.ds(base, WIN)]
                take(dve, added)
                dve.sem_inc(seg_free, 1)
                take(dve, seg_ready)
                dve.tensor_tensor(acc, acc, PS[:, bank + k % 2, 0:WIN], ALU.add).then_inc(added, 1)

                def further(i):
                    for q in range(TPC):
                        t = TPG * g + TPC * k + q
                        step(dve.tensor_scalar(ohx[:, q, :], iota_w[:, 0:WIN], win_off[:, bass.ds(i, 1)],
                                               dstT[:, bass.ds(t, 1)], ALU.add, ALU.is_equal))
                        if scaled:
                            step(dve.tensor_scalar(ohx[:, q, :], ohx[:, q, :], normT[:, bass.ds(t, 1)], None, ALU.mult))
                    dve.sem_inc(ohx_ready, 1)
                    take(dve, segx_ready)
                    accx = ACC[:, bass.ds(nc.s_assert_within(base + i * WIN, 0, N - 1, skip_runtime_bounds_check_because="no window starts past the greatest dst"), WIN)]
                    take(dve, added)
                    dve.tensor_tensor(accx, accx, PS[:, bank + 2, 0:WIN], ALU.add).then_inc(added, 1)
                further_windows(dve, reach, further)

            def count_hots(g, k):
                tiles = bass.ds(TPG * g + TPC * k, TPC)
                take(dve, cnt_done)
                dve.tensor_tensor(oh_lo[:, k % 2, :, :], over(iota_w[:, :], TPC, TNODES), each(loT[:, tiles], TNODES), ALU.is_equal)
                dve.tensor_tensor(oh_hi[:, k % 2, :, :], over(iota_h[:, :], TPC, NW), each(hiT[:, tiles], NW),
                                  ALU.is_equal).then_inc(cnt_oh, 1)

            def add_messages(g, h, use):
                for k in range(CPG):
                    nxt = after(g, h, use, k)
                    if nxt:
                        one_hots(nxt[0], nxt[3])
                        count_hots(nxt[0], nxt[3])
                    add_sums(g, k, 0, True)
                    dve.sem_inc(g_free, 1)
                dve.sem_inc(ix_free, 1)

            dve.sem_inc(cnt_done, 2)
            dve.sem_inc(seg_free, 1)
            dve.sem_inc(added, 1)
            one_hots(0, 0)
            count_hots(0, 0)
            by_pairs(dve, NG, add_messages)
            take(dve, added)
            take(dve, cnt_done, 2)
            take(dve, seg_free)

            def moments(u):
                for w in range(WPB):
                    dve.bn_stats(win(ln_st, u * WPB + w), win(X, u * WPB + w))

            def layer_norm_stats():
                dve.drain()
                m0, m1, v0, v1 = ln_st[:, :, 1], ln_st[:, :, 4], ln_st[:, :, 2], ln_st[:, :, 5]
                step(dve.tensor_tensor(ln_mv[:, :, 0], m0, m1, ALU.add))
                step(dve.tensor_scalar(ln_mv[:, :, 0], ln_mv[:, :, 0], 0.5, None, ALU.mult))
                step(dve.tensor_tensor(ln_mv[:, :, 1], m0, m1, ALU.subtract))
                step(dve.tensor_scalar(ln_mv[:, :, 1], ln_mv[:, :, 1], 0.5, None, ALU.mult))
                step(dve.tensor_tensor(ln_mv[:, :, 1], ln_mv[:, :, 1], ln_mv[:, :, 1], ALU.mult))
                step(dve.tensor_tensor(ln_r[:, :], v0, v1, ALU.add))
                step(dve.scalar_tensor_tensor(out=ln_mv[:, :, 1], in0=ln_r[:, :], scalar=1.0 / D, in1=ln_mv[:, :, 1],
                                              op0=ALU.mult, op1=ALU.add))
                step(dve.tensor_scalar(ln_mv[:, :, 1], ln_mv[:, :, 1], EPS, None, ALU.add))
                dve.sem_inc(var_ready, 1)
                take(dve, sd_ready)
                step(dve.reciprocal(ln_r[:, :], ln_r[:, :]))

            def normalise(u, s):
                for w in range(WPB):
                    v = u * WPB + w
                    ins = dve.tensor_scalar(xn[:, s, w * D:(w + 1) * D], win(X, v), ln_mv[:, bass.ds(v, 1), 0],
                                            ln_r[:, bass.ds(v, 1)], ALU.subtract, ALU.mult)
                return ins

            dve.sem_inc(accw_used, 2)

            def residual0(u, s, use):
                take(dve, sums_turned)
                dve.sem_inc(accw_ps, 1)
                xb = flat(X[:, bass.ds(u * WPB, WPB), :])
                step(dve.scalar_tensor_tensor(out=xb, in0=PS[:, s, :], scalar=0.0, in1=xb, op0=ALU.max, op1=ALU.add))
                dve.sem_inc(accw_used, 1)
                moments(u)
            by_pairs(dve, NBU, residual0)
            step(dve.memset(rcnt[:, :], 1.0))
            step(dve.tensor_scalar(rcnt[:, 0:NW], PS[:, 7, 0:NW], 1.0, None, ALU.max))
            step(dve.reciprocal(rcnt[:, :], rcnt[:, :]))
            layer_norm_stats()

            dve.sem_inc(a_split, 2)
            dve.sem_inc(xn_free, 2)

            def send_normal(u, s, use):
                take(dve, xn_free)
                step(normalise(u, s))
                dve.sem_inc(xn_kept, 1)
                dve.sem_inc(xn_ready, 1)

            def split_a(u, s, use):
                if not last(u, NBU):
                    send_normal(u + 1, 1 - s, use + s)
                take(dve, a_ps)
                if not first_use(use):
                    reached(dve, "dve", ast_out[s], 16 * use)
                ps = PS[:, 4 + s, :].rearrange("p (w d) -> p w d", w=WPB)
                res = resid[:, :].rearrange("p (w d) -> p w d", w=WPB)
                hi, mid, low = (ast[:, s, :, a, :] for a in range(3))
                step(dve.tensor_copy(hi, ps))
                step(dve.tensor_tensor(res, ps, hi, ALU.subtract))
                dve.sem_inc(a_split, 1)
                step(dve.tensor_copy(mid, res))
                step(dve.tensor_tensor(low, res, mid, ALU.subtract))
                dve.sem_inc(ast_ready, 1)
            send_normal(0, 0, 0)
            by_pairs(dve, NBU, split_a)
            take(dve, xn_free, 2)

            dve.sem_inc(dig_free, 2)
            dve.sem_inc(d_free, 2)
            dve.sem_inc(aw_free, CPG)
            dve.sem_inc(awx_free, 1)

            def look_up(k):
                take(dve, d_ready)
                dve.tensor_scalar(ohT[0:WIN, k % 2, :], PS[0:WIN, k % 2, :], node_col[0:WIN, 0:1], None, ALU.is_equal).then_inc(ohT_ready, 1)

            def first_moments(g, h, k):
                c = CPG * g + k
                take(dve, e_copied)
                cols = LASTC if last(c, NCH) else CHUNK
                dve.bn_stats(win(stats, c), stage[:, h, k * CHUNK:k * CHUNK + cols])

            def edge_features(g, h, use):
                for k in range(CPG):
                    nxt = after(g, h, use, k)
                    if nxt:
                        look_up(nxt[3])
                    reach = reach_of(dve, CPG * g + k)
                    take(dve, look_done)

                    def further(i):
                        dve.tensor_scalar(ohTx[0:WIN, :], PS[0:WIN, k % 2, :], node_col[0:WIN, bass.ds(i, 1)], None,
                                          ALU.is_equal).then_inc(ohTx_ready, 1)
                        take(dve, lookx_done)
                        dve.sem_inc(awx_free, 1)
                    further_windows(dve, reach, further)
                    for s in (d_free, g_free, aw_free, e_ready):
                        dve.sem_inc(s, 1)
                    if k == CPG - 1:
                        dve.sem_inc(dig_free, 1)
                        dve.sem_inc(ix_free, 1)
                    if k >= 1:
                        first_moments(g, h, k - 1)
                first_moments(g, h, CPG - 1)
                dve.drain().then_inc(e_measured, 1)
            look_up(0)
            by_pairs(dve, NG, edge_features)

            def scale_and_shift(at, g, b):
                dve.drain()
                step(dve.bn_aggr(small[:, at + 1:at + 3], flat(stats[:, :, :])))
                step(dve.tensor_scalar(small[:, at + 2:at + 3], small[:, at + 2:at + 3], EPS, None, ALU.add))
                dve.sem_inc(bn_var, 1)
                take(dve, bn_sd)
                step(dve.reciprocal(small[:, at + 4:at + 5], small[:, at + 3:at + 4]))
                step(dve.tensor_tensor(small[:, at + 5:at + 6], small[:, at + 4:at + 5], bn_in[:, g:g + 1], ALU.mult))
                step(dve.tensor_tensor(small[:, at + 7:at + 8], small[:, at + 1:at + 2], small[:, at + 5:at + 6], ALU.mult))
                step(dve.tensor_tensor(small[:, at + 6:at + 7], bn_in[:, b:b + 1], small[:, at + 7:at + 8], ALU.subtract))

            scale_and_shift(0, 0, 1)
            dve.sem_inc(e2_free, 2 * CPG)
            dve.sem_inc(bn0_ready, 1)

            def second_moments(g, h, use):
                for k in range(CPG):
                    c = CPG * g + k
                    take(dve, e2_ready)
                    cols = LASTC if last(c, NCH) else CHUNK
                    dve.bn_stats(win(stats, c), PS[:, CPG * h + k, 0:cols]).then_inc(e2_free, 1)
                dve.sem_inc(hot_free, 1)
            by_pairs(dve, NG, second_moments)
            dve.wait_ge(e2_free, 2 * CPG)
            scale_and_shift(8, 2, 3)
            step(dve.tensor_scalar(diag[:, :], fc1_s[:, :], small[:, 13:14], None, ALU.mult))
            step(dve.tensor_scalar(diag_t[:, :], ident[:, :], small[:, 14:15], None, ALU.mult))
            dve.sem_inc(fc1_scaled, 1)
            step(dve.memset(ACC[:, :], 0.0))
            step(dve.memset(shift3[:, :, :], 0.0))
            take(dve, fc1s_ps)
            step(dve.tensor_copy(fc1sT[:, :], PS[:, 0, 0:D]))
            shift_all, rest = resid[:, 0:D], resid[:, D:2 * D]
            part_all = oh_lo[:, 0, 0, :]
            step(dve.tensor_copy(shift_all, PS[:, 1, 0:D]))
            for a in range(3):
                step(dve.tensor_copy(part_all, shift_all))
                row = slice(32 * a, 32 * a + 1)
                step(dve.tensor_copy(shift3[row, :, :], part_all[row, :].rearrange("p (o d) -> p o d", o=1).to_broadcast([1, TPC, D])))
                if a < 2:
                    step(dve.tensor_tensor(rest, shift_all, part_all, ALU.subtract))
                    step(dve.tensor_copy(shift_all, rest))
            dve.sem_inc(r2_free, CPG)
            dve.sem_inc(oh_free, CPG)
            dve.sem_inc(pass3_go, 1)

            def sum_edges(g, h, use):
                for k in range(CPG):
                    add_sums(g, k, 4, False)
                    dve.sem_inc(r2_free, 1)
                    dve.sem_inc(oh_free, 1)
            dve.sem_inc(seg_free, 1)
            dve.sem_inc(added, 1)
            by_pairs(dve, NG, sum_edges)
            take(dve, added)

            def residual1(u, s, use):
                take(dve, sums_turned)
                dve.sem_inc(accw_ps, 1)
                for w in range(WPB):
                    v = u * WPB + w
                    ins = dve.scalar_tensor_tensor(out=resid[:, w * D:(w + 1) * D], in0=PS[:, s, w * D:(w + 1) * D],
                                                   scalar=rcnt[:, bass.ds(v, 1)], in1=win(X, v), op0=ALU.mult, op1=ALU.add)
                step(ins)
                dve.sem_inc(accw_used, 1)
                xb = flat(X[:, bass.ds(u * WPB, WPB), :])
                step(dve.scalar_tensor_tensor(out=xb, in0=resid[:, :], scalar=0.0, in1=xb, op0=ALU.max, op1=ALU.add))
                moments(u)
            by_pairs(dve, NBU, residual1)
            layer_norm_stats()

            def result(u, s, use):
                if not first_use(use):
                    reached(dve, "dve", res_out[s], 16 * use)
                normalise(u, s).then_inc(res_ready, 1)
            by_pairs(dve, NBU, result)


_INS = ['x', 'src', 'dst', 'edge_type_32', 'edge_weight1', 'L0_gnn_weight', 'L0_gnn_w_comp', 'L0_gnn_loop_weight',
        'L0_gnn_h_bias', 'L1_gnn_theta_w', 'L1_gnn_phi_w', 'L1_gnn_fc1_w', 'L1_gnn_bn0_g', 'L1_gnn_bn0_b',
        'L1_gnn_bn1_g', 'L1_gnn_bn1_b']


def kernel(**inputs):
    import numpy as np
    import concourse.bacc as bacc
    from concourse.bass_utils import run_bass_kernel_spmd as run

    nc = bacc.Bacc("TRN2", target_bir_lowering=False, num_devices=1)
    arrays, args = {}, []
    for name in _INS:
        a = np.ascontiguousarray(inputs[name])
        arrays[f"in_{name}"] = a
        args.append(nc.dram_tensor(f"in_{name}", a.shape, mybir.dt.from_np(a.dtype), kind="ExternalInput").ap())
    out = nc.dram_tensor("out_0", inputs["x"].shape, F32, kind="ExternalOutput").ap()
    gnn_kernel(nc, *args, out)
    return run(nc, [arrays], core_ids=[0]).results[0]["out_0"]
```

```python
from contextlib import ExitStack

import concourse.bass as bass
from concourse import mybir

P = 128
F32 = mybir.dt.float32
BF16 = mybir.dt.bfloat16
I32 = mybir.dt.int32
ALU = mybir.AluOpType
ACT = mybir.ActivationFunctionType
AX = mybir.AxisListType
EPS = 1e-5

D = 128
TILE = 128
TPC = 4
CHUNK = TILE * TPC
CPG = 4
TPG = TPC * CPG
GROUP = CHUNK * CPG
TNODES = 128
TNODES_BITS = 7
WIN = 80
TWIN = 24
WPB = 4
NK = P // TPC
SPAN = 1 << 13


def take(eng, sem, n=1):
    eng.wait_ge(sem, n)
    eng.sem_inc(sem, -n)


def flat(ap):
    return ap.rearrange("p a b -> p (a b)")


def over(ap, like, n):
    return ap.rearrange("p (o n) -> p o n", o=1).to_broadcast([P, like, n])


def each(ap, inner):
    p, n = ap.shape
    return ap.rearrange("p (n o) -> p n o", o=1).to_broadcast([p, n, inner])


def gnn_kernel(nc, x, src, dst, etype, norm, weight, w_comp, loop_w, h_bias,
               theta, phi, fc1, g0, b0, g1, b1, out):
    N = x.shape[0]
    E = src.shape[0]
    R, B = w_comp.shape
    NW = (N + TNODES - 1) // TNODES
    NXW = (N + WIN - 1) // WIN
    NTW = (N + TWIN - 1) // TWIN
    LASTN = N - (NW - 1) * TNODES
    NBU = (NW + WPB - 1) // WPB
    NWP = NBU * WPB
    NG = (E + GROUP - 1) // GROUP
    NCH = NG * CPG
    NB = (NG * TPG + P - 1) // P
    FULLB = E // (P * TILE)
    LROWS = E // TILE - FULLB * P
    LEDGE = E % TILE
    LASTC = E - (NCH - 1) * CHUNK
    ZW = B * TWIN
    EB = NB * TILE
    EVEN, ODD = NG - NG // 2, NG // 2
    assert NG % 2 == 1 and NBU % 2 == 1 and NW % 2 == 1
    assert 0 < LASTC <= CHUNK and FULLB == NB - 1 and LEDGE and NW > (NBU - 1) * WPB
    assert TPC * R == P and NW == NG

    ctx = ExitStack()

    def sb(name, shape, dt=F32):
        return ctx.enter_context(nc.sbuf_tensor(name, shape, dt))

    def sem(name):
        return ctx.enter_context(nc.semaphore(name))

    with ctx:
        atab = nc.dram_tensor("atab", [NWP * TNODES, 3 * D], BF16, kind="Internal").ap()
        btab = nc.dram_tensor("btab", [NWP * TNODES, D], F32, kind="Internal").ap()
        digits_d = nc.dram_tensor("digits_d", [2, NB * P * TILE], BF16, kind="Internal").ap()
        bounds_d = nc.dram_tensor("bounds_d", [NB, NK], I32, kind="Internal").ap()
        pairs_d = nc.dram_tensor("pairs_d", [NB, P // 2], I32, kind="Internal").ap()
        reaches_d = nc.dram_tensor("reaches_d", [NB, P], I32, kind="Internal").ap()
        wide_d = nc.dram_tensor("wide_d", [NB, P // TPG], I32, kind="Internal").ap()
        spill = nc.dram_tensor("spill", [NG, P, GROUP], F32, kind="Internal").ap()

        X = sb("X", [P, NWP, D])
        ACC = sb("ACC", [P, NWP * TNODES])
        iota_w = sb("iota_w", [P, TNODES])
        win_off0 = sb("win_off0", [P, NTW + 1])
        win_off = sb("win_off", [P, NXW + 1])
        node_col = sb("node_col", [P, NXW + 1])
        iota_h = sb("iota_h", [P, NW])
        ident = sb("ident", [P, P])
        identb = sb("identb", [P, P], BF16)
        rel_col = sb("rel_col", [P, 1])
        ones = sb("ones", [P, P])
        onesb = sb("onesb", [P, P], BF16)
        srcT = sb("srcT", [P, NB * P], I32)
        dst0T = sb("dst0T", [P, NB * P])
        dstT = sb("dstT", [P, NB * P])
        normT = sb("normT", [P, NB * P])
        hiT = sb("hiT", [P, NB * P])
        loT = sb("loT", [P, NB * P])
        bounds = sb("bounds", [1, NB * NK], I32)
        pairs = sb("pairs", [1, NB * P // 2], I32)
        reaches = sb("reaches", [1, NB * P], I32)
        wide = sb("wide", [1, NB * P // TPG], I32)
        ix = sb("ix", [P, 2, TPG], I32)
        G = sb("G", [P, 2, TPG, D])
        ohx = sb("ohx", [P, TPC, WIN])
        ohT = sb("ohT", [P, 2, CHUNK], BF16)
        ohTx = sb("ohTx", [P, CHUNK], BF16)
        oh_lo = sb("oh_lo", [P, 2, TPC, TNODES], BF16)
        oh_hi = sb("oh_hi", [P, 2, TPC, NW], BF16)
        small = sb("small", [P, 64])
        theta_s = sb("theta_s", [P, D])
        phi_s = sb("phi_s", [P, D])
        fc1_s = sb("fc1_s", [P, D])
        thph = sb("thph", [P, 2 * D])
        fc1T = sb("fc1T", [P, D])
        fc1sT = sb("fc1sT", [P, D])
        shift3 = sb("shift3", [96, TPC, D], BF16)
        diag = sb("diag", [P, D])
        diag_t = sb("diag_t", [P, D])
        loop_s = sb("loop_s", [P, D])
        bn_in = sb("bn_in", [P, 5])
        stats = sb("stats", [P, NCH, 6])
        ln_st = sb("ln_st", [P, NWP, 6])
        ln_mv = sb("ln_mv", [P, NWP, 2])
        ln_r = sb("ln_r", [P, NWP])
        rcnt = sb("rcnt", [P, NWP])
        xn = sb("xn", [P, 2, WPB * D])
        xT = sb("xT", [P, 2, WPB * D])
        bst = sb("bst", [P, 2, WPB * D])
        resid = sb("resid", [P, WPB * D])
        BIG_N = 15 * 1024
        BIG = sb("BIG", [P, BIG_N])
        at = [0]

        def part(n):
            at[0] += n
            assert at[0] <= BIG_N
            return BIG[:, at[0] - n:at[0]]
        stage = part(2 * GROUP).rearrange("p (s n) -> p s n", s=2)
        R2 = part(CPG * CHUNK).rearrange("p (s q d) -> p s q d", s=CPG, q=TPC)
        oh3 = part(GROUP)
        digits = oh3[0:2, :].bitcast(BF16).rearrange("p (s n) -> p s n", s=2)
        oh3 = oh3[:, 0:CPG * TPC * WIN].rearrange("p (s q n) -> p s q n", s=CPG, q=TPC)
        ast = part(WPB * 3 * D).bitcast(BF16).rearrange("p (s w a d) -> p s w a d", s=2, w=WPB, a=3)
        aw = part(CPG * 3 * D // 2).bitcast(BF16).rearrange("p (s a d) -> p s a d", s=CPG, a=3)
        dst_g = part(2 * TPG).rearrange("p (s t) -> p s t", s=2)
        awx = part(3 * D // 2).bitcast(BF16).rearrange("p (a d) -> p a d", a=3)
        hot = G[:, :, :, :].rearrange("p s t d -> p s (t d)")

        at[0] = 0
        coef = part(NB * P * B).rearrange("p (b t k) -> p b t k", b=NB, k=B)
        soh = part(CPG * TPC * ZW).rearrange("p (s q k n) -> p s q k n", s=CPG, q=TPC, k=B)
        zs = part(2 * TPC * ZW).rearrange("p (s q k n) -> p s q k n", s=2, q=TPC, k=B)
        sohx = part(ZW).rearrange("p (k n) -> p k n", k=B)
        zsx = part(ZW).rearrange("p (k n) -> p k n", k=B)
        gx = part(D)
        basis = part(B * D).rearrange("p (k f) -> p k f", k=B)
        rel_oh = part(NB * TILE).bitcast(BF16).rearrange("p (s n) -> p s n", s=2)
        typ_b = part(NB * TILE // 2).bitcast(BF16).rearrange("p (b e) -> p b e", b=NB)
        typ_s = flat(zs[:, :, :, :, :].rearrange("p s q k n -> p s (q k n)"))[:, 0:NB * TILE].bitcast(BF16)\
            .rearrange("p (s n) -> p s n", s=2)
        wbd = part(TPC * B)
        wbd_r = part(TPC * B)
        wbd_p = part(3 * TPC * B // 2).bitcast(BF16).rearrange("p (a n) -> p a n", a=3)
        sel = part(P).bitcast(BF16).rearrange("p (s n) -> p s n", s=2)
        p_int = part(2).bitcast(I32)

        xf, accf = flat(X[:, :, :]), ACC[:, :]

        def rows(of, k, dt=F32):
            v = of[:, EB * k:EB * (k + 1)]
            return (v if dt is F32 else v.bitcast(dt)).rearrange("p (b e) -> p b e", b=NB)
        r_src, r_typ, r_dst = (rows(xf, k, I32) for k in range(3))
        r_nrm, f_src, f_rel0, f_rel = (rows(xf, k) for k in range(3, 7))
        f_hi, f_lo, f_dst, f_min = (rows(accf, k) for k in range(4))
        a_hi, i_rel, i_hi = (rows(accf, k, I32) for k in range(4, 7))
        digs = flat(bst[:, :, :])
        dig_hi, dig_lo = (digs[:, k * EB // 2:(k + 1) * EB // 2].bitcast(BF16).rearrange("p (b e) -> p b e", b=NB)
                          for k in range(2))
        t_min, t_max, t_base, t_first = (part(NB) for _ in range(4))
        c_min, c_max = (part(NK)[0:NB, :] for _ in range(2))
        c_ext = part(2 * NK)[0:NB, :].bitcast(I32)
        c_win = part(NK)[0:NB, :].bitcast(I32)
        c_tile, e_min, e_ext = (xT[0:NB, 0, P * k:P * (k + 1)] for k in range(3))
        e_int = xn[0:NB, 0, 0:2 * P].bitcast(I32)
        e_reach = xn[0:NB, 0, 2 * P:3 * P].bitcast(I32)
        e_wide = xn[0:NB, 0, 3 * P:3 * P + P // TPG].bitcast(I32)
        e_pair = xn[0:NB, 1, 0:P // 2].bitcast(mybir.dt.int16)

        PS = ctx.enter_context(nc.psum_tensor("PS", [P, 8, 512], F32))

        const_done = sem("const_done")
        pads_set = sem("pads_set")
        x_in = sem("x_in")
        edges_in = {v: sem(f"{v}_rows_in") for v in ("src", "dst", "typ", "norm")}
        wcomp_in = sem("wcomp_in")
        wbd_zero = sem("wbd_zero")
        wts_in = sem("wts_in")
        dve_self = sem("dve_self")
        act_self = sem("act_self")
        pool_self = sem("pool_self")
        src_rows = sem("src_rows")
        rel0_rows = sem("rel0_rows")
        rel_rows = sem("rel_rows")
        hi_rows = sem("hi_rows")
        lo_rows = sem("lo_rows")
        typ_rows = sem("typ_rows")
        coef_consts = sem("coef_consts")
        sel_ready = sem("sel_ready")
        typ_s_ready = sem("typ_s_ready")
        typ_s_free = sem("typ_s_free")
        typ_ps = sem("typ_ps")
        rel_oh_ready = sem("rel_oh_ready")
        coef_ps = sem("coef_ps")
        coef_free = sem("coef_free")
        rows_used = sem("rows_used")
        acc_zero = sem("acc_zero")
        group_in = sem("group_in")
        setup_out = sem("setup_out")
        rows_out = sem("rows_out")
        minmax = sem("minmax")
        minmax_T = sem("minmax_T")
        base_rows = sem("base_rows")
        base_T = sem("base_T")
        bnd_in = sem("bnd_in")
        rows_T = sem("rows_T")
        cols_ready = sem("cols_ready")
        wT_ps = sem("wT_ps")
        wT_done = sem("wT_done")
        xwin_ready = sem("xwin_ready")
        xwT_ps = sem("xwT_ps")
        xwT_ready = sem("xwT_ready")
        loop_ps = sem("loop_ps")
        loop_done = sem("loop_done")
        z_ready = sem("z_ready")
        z_copied = sem("z_copied")
        zx_ready = sem("zx_ready")
        sums_done = sem("sums_done")
        zx_copied = sem("zx_copied")
        ix_ready = sem("ix_ready")
        ix_free = sem("ix_free")
        gathered = [sem(f"gathered{i}") for i in range(2 * CPG)]
        g_free = sem("g_free")
        oh_ready = sem("oh_ready")
        oh_free = sem("oh_free")
        seg_ready = sem("seg_ready")
        seg_free = sem("seg_free")
        ohx_ready = sem("ohx_ready")
        segx_ready = sem("segx_ready")
        added = sem("added")
        cnt_oh = sem("cnt_oh")
        cnt_done = sem("cnt_done")
        ticks = {e: sem(f"tick_{e}") for e in ("pe", "act", "sp", "pool", "dve")}
        accw_ready = sem("accw_ready")
        accw_ps = sem("accw_ps")
        sums_turned = sem("sums_turned")
        accw_used = sem("accw_used")
        var_ready = sem("var_ready")
        sd_ready = sem("sd_ready")
        xn_ready = sem("xn_ready")
        xn_kept = sem("xn_kept")
        xn_free = sem("xn_free")
        nT_ps = sem("nT_ps")
        nT_ready = sem("nT_ready")
        a_ps = sem("a_ps")
        b_ps = sem("b_ps")
        b_copied = sem("b_copied")
        a_split = sem("a_split")
        ast_ready = sem("ast_ready")
        bst_ready = sem("bst_ready")
        ast_out = [sem("ast_out0"), sem("ast_out1")]
        bst_out = [sem("bst_out0"), sem("bst_out1")]
        tabs_done = sem("tabs_done")
        dig_in = [sem("dig_in0"), sem("dig_in1")]
        dig_free = sem("dig_free")
        aw_in = [sem(f"aw_in{k}") for k in range(CPG)]
        aw_free = sem("aw_free")
        awx_in = sem("awx_in")
        awx_free = sem("awx_free")
        d_ready = sem("d_ready")
        d_free = sem("d_free")
        ohT_ready = sem("ohT_ready")
        look_done = sem("look_done")
        ohTx_ready = sem("ohTx_ready")
        lookx_done = sem("lookx_done")
        e_ready = sem("e_ready")
        e_free = sem("e_free")
        e_copied = sem("e_copied")
        e_measured = sem("e_measured")
        stored = [sem("stored0"), sem("stored1")]
        bn0_ready = sem("bn0_ready")
        st_in = [sem("st_in0"), sem("st_in1")]
        st_free = sem("st_free")
        hot_ready = sem("hot_ready")
        hot_free = sem("hot_free")
        e2_ready = sem("e2_ready")
        e2_free = sem("e2_free")
        bn_var = sem("bn_var")
        bn_sd = sem("bn_sd")
        fc1_scaled = sem("fc1_scaled")
        fc1s_ps = sem("fc1s_ps")
        pass3_go = sem("pass3_go")
        y_ready = sem("y_ready")
        r2_ready = sem("r2_ready")
        r2_free = sem("r2_free")
        res_ready = sem("res_ready")
        res_out = [sem("res_out0"), sem("res_out1")]

        def reached(eng, name, s, value):
            eng.wait_ge(s, value)
            eng.sem_inc(ticks[name], 1)

        def by_pairs(eng, n, body):
            body(0, 0, 0)
            body(1, 1, 0)
            with eng.Fori(1, n // 2) as i:
                body(2 * i, 0, i)
                body(2 * i + 1, 1, i)
            body(n - 1, 0, n // 2)

        def first_use(use):
            return isinstance(use, int) and use == 0

        def last(i, n):
            return isinstance(i, int) and i == n - 1

        def after(g, h, use, k):
            if k + 1 < CPG:
                return g, h, use, k + 1
            if last(g, NG):
                return None
            return g + 1, 1 - h, use + h, 0

        def reach_of(eng, c):
            return eng.value_load(bounds[0:1, bass.ds(c, 1)], min_val=SPAN, max_val=SPAN * (NXW + 1) - 1)

        def pair_of(eng, t):
            v = eng.value_load(pairs[0:1, bass.ds(t // 2, 1)], min_val=0, max_val=(N - 1) * ((1 << 16) + 1))
            return tuple(nc.s_assert_within(b, 0, N - 1, skip_runtime_bounds_check_because="it is a node")
                         for b in (v % (1 << 16), v // (1 << 16)))

        def tile_windows(eng, g, body, before):
            with eng.If(eng.value_load(wide[0:1, bass.ds(g, 1)], min_val=0, max_val=NTW) >= 1):
                before()
                with eng.Fori(0, TPG) as j:
                    reach = eng.value_load(reaches[0:1, bass.ds(TPG * g + j, 1)], min_val=SPAN, max_val=SPAN * (NTW + 1) - 1)
                    body(j, reach)

        def least_dst(eng, reach):
            return nc.s_assert_within(reach % SPAN, 0, N - 1, skip_runtime_bounds_check_because="it is a node")

        def further_windows(eng, reach, body):
            with eng.If(reach >= 2 * SPAN):
                with eng.Fori(1, reach // SPAN) as i:
                    body(i)

        def win(t, w):
            return t[:, bass.ds(w, 1), :].rearrange("p o d -> p (o d)")

        block = ctx.enter_context(nc.Block())

        @block.sync
        def _(sp):
            sp.wait_ge(pads_set, 4)
            norm_v = norm.rearrange("e o -> (e o)")
            at_e = FULLB * P * TILE
            for name, vec, r in (("src", src, r_src), ("dst", dst, r_dst), ("typ", etype, r_typ), ("norm", norm_v, r_nrm)):
                sp.dma_start(r[:, 0:FULLB, :], vec[0:at_e].rearrange("(b p e) -> p b e", p=P, e=TILE)).then_inc(edges_in[name], 16)
                sp.dma_start(r[0:LROWS, FULLB, :],
                             vec[at_e:at_e + LROWS * TILE].rearrange("(p e) -> p e", e=TILE)).then_inc(edges_in[name], 16)
                sp.dma_start(r[LROWS:LROWS + 1, FULLB, 0:LEDGE],
                             vec[E - LEDGE:E].rearrange("(p e) -> p e", p=1)).then_inc(edges_in[name], 16)
            sp.wait_ge(wbd_zero, 1)
            for q in range(TPC):
                sp.dma_start(wbd[q * R:(q + 1) * R, q * B:(q + 1) * B], w_comp).then_inc(wcomp_in, 16)
            sp.dma_start(basis, weight.rearrange("b d f -> d b f")).then_inc(wts_in, 16)
            for a, t in ((loop_s, loop_w), (theta_s, theta), (phi_s, phi), (fc1_s, fc1)):
                sp.dma_start(a[:, :], t).then_inc(wts_in, 16)
            for k, v in enumerate((g0, b0, g1, b1, h_bias)):
                sp.dma_start(bn_in[:, k:k + 1], v.rearrange("(f o) -> f o", o=1)).then_inc(wts_in, 16)
            sp.wait_ge(setup_out, 3)
            sp.dma_start(bounds_d[:, :], c_win).then_inc(rows_out, 16)
            sp.dma_start(pairs_d[:, :], e_pair.bitcast(I32)).then_inc(rows_out, 16)
            sp.dma_start(reaches_d[:, :], e_reach).then_inc(rows_out, 16)
            sp.dma_start(wide_d[:, :], e_wide).then_inc(rows_out, 16)
            for k, dg in enumerate((dig_hi, dig_lo)):
                sp.dma_start(digits_d[k, :].rearrange("(b p e) -> p b e", p=P, e=TILE), dg).then_inc(rows_out, 16)
            sp.wait_ge(rows_out, 16 * 6)
            for to, of in ((bounds, bounds_d), (pairs, pairs_d), (reaches, reaches_d), (wide, wide_d)):
                sp.dma_start(to[:, :], of.rearrange("(o b) c -> o (b c)", o=1)).then_inc(bnd_in, 16)
            sp.wait_ge(rows_used, 1)
            sp.dma_start(X[:, 0:NW - 1, :], x[0:(NW - 1) * TNODES, :].rearrange("(w p) d -> p w d", p=P)).then_inc(x_in, 16)
            sp.dma_start(X[0:LASTN, NW - 1, :], x[(NW - 1) * TNODES:N, :]).then_inc(x_in, 16)

            def store_tables(u, s, use):
                rows_u = bass.ds(u * (WPB * TNODES), WPB * TNODES)
                take(sp, bst_ready)
                sp.dma_start(btab[rows_u, :].rearrange("(w p) d -> p w d", p=P),
                             bst[:, s, :].rearrange("p (w d) -> p w d", w=WPB)).then_inc(bst_out[s], 16)
                take(sp, ast_ready)
                sp.dma_start(atab[rows_u, :].rearrange("(w p) n -> p w n", p=P),
                             ast[:, s, :, :, :].rearrange("p w a d -> p w (a d)")).then_inc(ast_out[s], 16)
            by_pairs(sp, NBU, store_tables)
            for o in (ast_out, bst_out):
                sp.wait_ge(o[0], 16 * (NBU - NBU // 2))
                sp.wait_ge(o[1], 16 * (NBU // 2))
            sp.sem_inc(tabs_done, 1)

            def load_digits(g, h):
                take(sp, dig_free)
                sp.dma_start(digits[:, h, :], digits_d[:, bass.ds(g * GROUP, GROUP)]).then_inc(dig_in[h], 16)

            def load_windows(g, h, use):
                for k in range(CPG):
                    if k == CPG // 2 and not last(g, NG):
                        load_digits(g + 1, 1 - h)
                    reach = reach_of(sp, CPG * g + k)
                    base = least_dst(sp, reach)
                    take(sp, aw_free)
                    sp.dma_start(aw[0:WIN, k, :, :].rearrange("p a d -> p (a d)"), atab[bass.ds(base, WIN), :]).then_inc(aw_in[k], 16)

                    def further(i):
                        take(sp, awx_free)
                        at_w = nc.s_assert_within(base + i * WIN, 0, N - 1, skip_runtime_bounds_check_because="no window starts past the greatest dst")
                        sp.dma_start(awx[0:WIN].rearrange("p a d -> p (a d)"), atab[bass.ds(at_w, WIN), :]).then_inc(awx_in, 16)
                    further_windows(sp, reach, further)
            load_digits(0, 0)
            by_pairs(sp, NG, load_windows)

            sp.wait_ge(stored[0], 16 * EVEN)
            sp.wait_ge(stored[1], 16 * ODD)

            def load_e(g, h, use):
                take(sp, st_free)
                sp.dma_start(stage[:, h, :], spill[bass.ds(g, 1), :, :].rearrange("o p n -> (o p) n")).then_inc(st_in[h], 16)
            for _ in range(2):
                take(sp, st_free, 2)
                sp.sem_inc(st_free, 2)
                by_pairs(sp, NG, load_e)

            def store_out(u, s, use):
                take(sp, res_ready)
                r = xn[:, s, :].rearrange("p (w d) -> p w d", w=WPB)
                if last(u, NBU):
                    full = NW - 1 - WPB * u
                    if full:
                        sp.dma_start(out[u * WPB * TNODES:(NW - 1) * TNODES, :].rearrange("(w p) d -> p w d", p=P),
                                     r[:, 0:full, :]).then_inc(res_out[s], 16)
                    sp.dma_start(out[(NW - 1) * TNODES:N, :], r[0:LASTN, full, :]).then_inc(res_out[s], 16)
                    sp.wait_ge(res_out[s], 16 * (use + 1 + (full > 0)))
                else:
                    sp.dma_start(out[bass.ds(u * (WPB * TNODES), WPB * TNODES), :].rearrange("(w p) d -> p w d", p=P), r)\
                      .then_inc(res_out[s], 16)
            by_pairs(sp, NBU, store_out)
            sp.wait_ge(res_out[1], 16 * (NBU // 2))

        @block.gpsimd
        def _(pool):
            nc.gpsimd.memset(r_dst[:, FULLB, :], -1).then_inc(pads_set, 1)
            nc.gpsimd.memset(r_src[:, FULLB, :], 0).then_inc(pads_set, 1)
            nc.gpsimd.memset(r_typ[:, FULLB, :], 0).then_inc(pads_set, 1)
            nc.gpsimd.memset(r_nrm[:, FULLB, :], 0.0).then_inc(pads_set, 1)
            nc.gpsimd.memset(ones[:, :], 1.0).then_inc(const_done, 1)
            nc.gpsimd.memset(onesb[:, :], 1.0).then_inc(const_done, 1)
            nc.gpsimd.memset(ident[:, :], 0.0).then_inc(const_done, 1)
            pool.wait_ge(const_done, 3)
            nc.gpsimd.affine_select(out=ident[:, :], in_=ident[:, :], compare_op=ALU.not_equal, fill=1.0, base=0,
                                    pattern=[[-1, P]], channel_multiplier=1).then_inc(const_done, 1)
            for t, step, n, cm in ((iota_w, 1, TNODES, 0), (win_off, WIN, NXW + 1, 0), (win_off0, TWIN, NTW + 1, 0), (node_col, WIN, NXW + 1, 1), (iota_h, 1, NW, 0)):
                nc.gpsimd.iota(t[:, :], pattern=[[step, n]], base=0, channel_multiplier=cm,
                               allow_small_or_imprecise_dtypes=True).then_inc(const_done, 1)
            nc.gpsimd.memset(wbd, 0.0).then_inc(wbd_zero, 1)
            pool.sem_inc(g_free, 2 * CPG)
            pool.sem_inc(ix_free, 2)

            def gathers(rows_of, meanwhile=None):
                def one(g, h, use):
                    take(pool, ix_ready)
                    for k in range(CPG):
                        take(pool, g_free)
                        for q in range(TPC):
                            t = TPC * k + q
                            nc.gpsimd.indirect_dma_start(
                                out=G[:, h, t, :], out_offset=None, in_=rows_of,
                                in_offset=bass.IndirectOffsetOnAxis(ap=ix[:, h, t:t + 1], axis=0),
                            ).then_inc(gathered[CPG * h + k], 16)
                    if meanwhile and isinstance(g, int) and g == 1:
                        meanwhile()
                by_pairs(pool, NG, one)

            def zero_sums():
                pool.wait_ge(rows_used, 1)
                nc.gpsimd.memset(ACC[:, :], 0.0).then_inc(acc_zero, 1)
            gathers(x, zero_sums)

            def keep(u, s, use):
                take(pool, xn_kept)
                nc.gpsimd.tensor_copy(flat(X[:, bass.ds(u * WPB, WPB), :]), xn[:, s, :]).then_inc(xn_free, 1)
            by_pairs(pool, NBU, keep)

            pool.wait_ge(tabs_done, 1)
            gathers(btab[:, :])
            nc.gpsimd.memset(ACC[:, :], 0.0).then_inc(acc_zero, 1)

            pool.wait_ge(pass3_go, 1)

            def one_hots(g, h, use):
                nc.gpsimd.tensor_copy(dst_g[:, h, :], dstT[:, bass.ds(TPG * g, TPG)]).then_inc(pool_self, 1)
                take(pool, pool_self)
                for k in range(CPG):
                    take(pool, oh_free)
                    for q in range(TPC):
                        t = TPC * k + q
                        ins = nc.gpsimd.tensor_scalar(oh3[:, k, q, :], iota_w[:, 0:WIN], dst_g[:, h, t:t + 1], None, ALU.is_equal)
                    ins.then_inc(oh_ready, 1)
            by_pairs(pool, NG, one_hots)

        @block.tensor
        def _(pe):
            pe.wait_ge(const_done, 9)
            arrays = iter(range(6))

            def to_columns(f):
                k = next(arrays)
                if k >= 3:
                    pe.wait_ge(cols_ready, k - 2)
                for b in range(NB):
                    mm = pe.transpose(PS[:, 2 + 2 * (k % 3) + b // 4, (b % 4) * P:(b % 4 + 1) * P], f[:, b, :], ident[:, :])
                mm.then_inc(rows_T, 1)
            pe.wait_ge(src_rows, 1)
            to_columns(f_src)
            pe.wait_ge(minmax, 1)
            pe.transpose(PS[0:NB, 0, 0:P], t_min, ident[:, :])
            pe.transpose(PS[0:NB, 0, P:2 * P], t_max, ident[:, :]).then_inc(minmax_T, 1)
            pe.wait_ge(rel0_rows, 1)
            to_columns(f_rel0)
            pe.wait_ge(edges_in["norm"], 48)
            to_columns(r_nrm)
            take(pe, base_rows)
            pe.transpose(PS[:, 1, 0:NB], c_tile, ident[0:NB, 0:NB]).then_inc(base_T, 1)
            for f, ready in ((f_rel, rel_rows), (f_hi, hi_rows), (f_lo, lo_rows)):
                pe.wait_ge(ready, 1)
                to_columns(f)
            pe.wait_ge(wts_in, 16 * 10)
            pe.wait_ge(cols_ready, 6)
            for k, a in enumerate((theta_s, phi_s, fc1_s)):
                mm = pe.transpose(PS[:, 6, k * D:(k + 1) * D], a[:, :], ident[:, :])
            mm.then_inc(wT_ps, 1)

            pe.wait_ge(coef_consts, 1)
            pe.wait_ge(typ_rows, 1)

            def spread_types(s):
                take(pe, sel_ready)
                pe.matmul(PS[:, 2 * s, :], sel[:, s, :], typ_b[:, 0:4, :], start=True, stop=True)
                pe.matmul(PS[:, 2 * s + 1, 0:(NB - 4) * TILE], sel[:, s, :], typ_b[:, 4:NB, :], start=True, stop=True).then_inc(typ_ps, 1)

            def look_up_coef(s):
                take(pe, coef_free)
                take(pe, rel_oh_ready)
                for b in range(NB):
                    for a in range(3):
                        mm = pe.matmul(PS[:, 4 + s, b * TPC * B:(b + 1) * TPC * B], rel_oh[:, s, b * TILE:(b + 1) * TILE],
                                       wbd_p[:, a, :], start=(a == 0), stop=(a == 2), skip_group_check=True)
                mm.then_inc(coef_ps, 1)
            pe.wait_ge(wT_done, 1)
            spread_types(0)
            spread_types(1)
            with pe.Fori(0, NK // 2 - 1):
                for s in range(2):
                    spread_types(s)
                    look_up_coef(s)
            look_up_coef(0)
            look_up_coef(1)

            take(pe, coef_free, 2)
            pe.wait_ge(bnd_in, 64)

            def scaled_sums(g, h, use, k):
                reached(pe, "pe", gathered[CPG * h + k], 16 * TPC * (use + 1))
                if k == CPG - 1:
                    pe.sem_inc(ix_free, 1)
                take(pe, oh_ready)
                for q in range(TPC):
                    mm = pe.matmul(PS[:, 2 * (k % 2) + q // 2, (q % 2) * ZW:(q % 2 + 1) * ZW], G[:, h, TPC * k + q, :],
                                   soh[:, k, q, :, :].rearrange("p k n -> p (k n)"), start=True, stop=True)
                mm.then_inc(z_ready, 1)

            def add_messages(g, h, use):
                def whole_group():
                    for k in range(CPG):
                        reached(pe, "pe", gathered[CPG * h + k], 16 * TPC * (use + 1))
                    pe.sem_inc(group_in, 1)

                def tile(j, reach):
                    def further(i):
                        take(pe, ohx_ready)
                        pe.matmul(PS[:, 6, 0:ZW], gx, sohx.rearrange("p k n -> p (k n)"), start=True, stop=True).then_inc(zx_ready, 1)
                        take(pe, zx_copied)
                        for b in range(B):
                            mm = pe.matmul(PS[:, 6, ZW:ZW + TWIN], basis[:, b, :], zsx[:, b, :], start=(b == 0), stop=(b == B - 1))
                        mm.then_inc(segx_ready, 1)
                    further_windows(pe, reach, further)
                tile_windows(pe, g, tile, whole_group)
                for k in range(CPG):
                    nxt = after(g, h, use, k)
                    if nxt:
                        scaled_sums(*nxt)
                    take(pe, z_copied)
                    take(pe, seg_free)
                    for b in range(B):
                        mm = pe.matmul(PS[:, 4 + k % 2, 0:TPC * TWIN], basis[:, b, :], zs[:, k % 2, :, b, :],
                                       start=(b == 0), stop=(b == B - 1))
                    mm.then_inc(seg_ready, 1)
                    if k == 1:
                        take(pe, xwin_ready)
                        take(pe, loop_done)
                        pe.transpose(PS[:, 7, 0:P], xn[:, h, 0:D], ident[:, :]).then_inc(xwT_ps, 1)
                    if k == 3:
                        take(pe, xwT_ready)
                        pe.matmul(PS[:, 7, P:2 * P], loop_s[:, :], xT[:, h, 0:D], start=True, stop=True).then_inc(loop_ps, 1)

            scaled_sums(0, 0, 0, 0)
            by_pairs(pe, NG, add_messages)

            def turn_sums(u, s, use):
                take(pe, accw_ready)
                take(pe, accw_used)
                for w in range(WPB):
                    mm = pe.transpose(PS[:, s, w * D:(w + 1) * D], xT[:, s, w * D:(w + 1) * D], ident[:, :])
                mm.then_inc(sums_turned, 1)
            by_pairs(pe, NBU, turn_sums)

            def node_tables(u, s, use):
                take(pe, xn_ready)
                for w in range(WPB):
                    mm = pe.transpose(PS[:, 2 + s, w * D:(w + 1) * D], xn[:, s, w * D:(w + 1) * D], ident[:, :])
                mm.then_inc(nT_ps, 1)
                take(pe, nT_ready)
                for half, bank, free, full in ((0, 4 + s, a_split, a_ps), (1, 6 + s, b_copied, b_ps)):
                    take(pe, free)
                    for w in range(WPB):
                        mm = pe.matmul(PS[:, bank, w * D:(w + 1) * D], xT[:, s, w * D:(w + 1) * D],
                                       thph[:, half * D:(half + 1) * D], start=(w == 0), stop=(w == WPB - 1), skip_group_check=True)
                    mm.then_inc(full, 1)
            by_pairs(pe, NBU, node_tables)

            def spread_dst(g, h, use, k):
                if k == 0:
                    reached(pe, "pe", dig_in[h], 16 * (use + 1))
                take(pe, d_free)
                pe.matmul(PS[:, k % 2, :], onesb[0:2, :], digits[:, h, k * CHUNK:(k + 1) * CHUNK],
                          start=True, stop=True).then_inc(d_ready, 1)

            def edge_features(g, h, use):
                for k in range(CPG):
                    reach = reach_of(pe, CPG * g + k)
                    reached(pe, "pe", gathered[CPG * h + k], 16 * TPC * (use + 1 + (EVEN, ODD)[h]))
                    take(pe, e_free)
                    for q in range(TPC):
                        pe.matmul(PS[:, 2 + k % 2, q * TILE:(q + 1) * TILE], G[:, h, TPC * k + q, :], ident[:, :],
                                  start=(q == 0), stop=False, skip_group_check=True)
                    nxt = after(g, h, use, k)
                    if nxt:
                        spread_dst(*nxt)
                    reached(pe, "pe", aw_in[k], 16 * (g + 1))
                    take(pe, ohT_ready)
                    for a in range(3):
                        mm = pe.matmul(PS[:, 2 + k % 2, :], aw[0:WIN, k, a, :], ohT[0:WIN, k % 2, :],
                                       start=False, stop=(a == 2), skip_group_check=True)
                    mm.then_inc(look_done, 1)
                    take(pe, cnt_oh)
                    for q in range(TPC):
                        mm = pe.matmul(PS[:, 7, 0:NW], oh_lo[:, k % 2, q, :], oh_hi[:, k % 2, q, :],
                                       start=(isinstance(g, int) and g == 0 and k == 0 and q == 0),
                                       stop=(last(g, NG) and k == CPG - 1 and q == TPC - 1), skip_group_check=True)
                    mm.then_inc(cnt_done, 1)

                    def further(i):
                        take(pe, awx_in, 16)
                        take(pe, ohTx_ready)
                        for a in range(3):
                            mm = pe.matmul(PS[:, 2 + k % 2, :], awx[0:WIN, a, :], ohTx[0:WIN, :],
                                           start=False, stop=(a == 2), skip_group_check=True)
                        mm.then_inc(lookx_done, 1)
                    further_windows(pe, reach, further)
            spread_dst(0, 0, 0, 0)
            by_pairs(pe, NG, edge_features)

            def second_product(g, h, use):
                take(pe, hot_ready)
                pe.sem_inc(st_free, 1)
                for k in range(CPG):
                    take(pe, e2_free)
                    pe.matmul(PS[:, CPG * h + k, :], fc1T[:, :], hot[:, h, k * CHUNK:(k + 1) * CHUNK],
                              start=True, stop=True).then_inc(e2_ready, 1)
            by_pairs(pe, NG, second_product)

            take(pe, fc1_scaled)
            pe.transpose(PS[:, 0, 0:D], diag[:, :], ident[:, :])
            pe.matmul(PS[:, 1, 0:D], ones[:, :], diag_t[:, :], start=True, stop=True).then_inc(fc1s_ps, 1)
            pe.wait_ge(pass3_go, 1)

            def second_again(g, h, use, k):
                take(pe, hot_ready)
                if k == CPG - 1:
                    pe.sem_inc(st_free, 1)
                pe.matmul(PS[:, k, :], onesb[0:96, :], shift3[:, :, :].rearrange("p q d -> p (q d)"),
                          start=True, stop=False, skip_group_check=True)
                for q in range(TPC):
                    t = TPC * k + q
                    mm = pe.matmul(PS[:, k, q * D:(q + 1) * D], hot[:, h, t * TILE:(t + 1) * TILE], fc1sT[:, :],
                                   start=False, stop=(q == TPC - 1), skip_group_check=True)
                mm.then_inc(y_ready, 1)

            def sum_edges(g, h, use):
                for k in range(CPG):
                    nxt = (g, h, use, k)
                    for _ in range(3):
                        nxt = nxt and after(*nxt)
                    if nxt:
                        second_again(*nxt)
                    take(pe, r2_ready)
                    take(pe, seg_free)
                    take(pe, oh_ready)
                    for q in range(TPC):
                        mm = pe.matmul(PS[:, 4 + k % 2, 0:WIN], R2[:, k, q, :], oh3[:, k, q, :],
                                       start=(q == 0), stop=(q == TPC - 1))
                    mm.then_inc(seg_ready, 1)

                    def further(i):
                        take(pe, ohx_ready)
                        for q in range(TPC):
                            mm = pe.matmul(PS[:, 6, 0:WIN], R2[:, k, q, :], ohx[:, q, :],
                                           start=(q == 0), stop=(q == TPC - 1))
                        mm.then_inc(segx_ready, 1)
                    further_windows(pe, reach_of(pe, CPG * g + k), further)
            second_again(0, 0, 0, 0)
            second_again(0, 0, 0, 1)
            second_again(0, 0, 0, 2)
            by_pairs(pe, NG, sum_edges)
            by_pairs(pe, NBU, turn_sums)

        @block.scalar
        def _(act):
            act.wait_ge(const_done, 9)
            act.wait_ge(edges_in["src"], 48)
            act.activation(f_src, r_src, ACT.Copy).then_inc(src_rows, 1)

            def columns(k, to):
                act.wait_ge(rows_T, k + 1)
                at_b = 2 + 2 * (k % 3)
                act.activation(to[:, :], flat(PS[:, at_b:at_b + 2, :])[:, 0:NB * P], ACT.Copy).then_inc(cols_ready, 1)
            columns(0, srcT)
            act.wait_ge(cols_ready, 1)
            for h in range(2):
                take(act, ix_free)
                act.activation(ix[:, h, :], srcT[:, h * TPG:(h + 1) * TPG], ACT.Copy).then_inc(ix_ready, 1)
            act.wait_ge(edges_in["typ"], 48)
            act.activation(typ_b, r_typ, ACT.Copy).then_inc(typ_rows, 1)
            for k, to in enumerate((dst0T, normT, dstT, hiT, loT)):
                columns(k + 1, to)

            def select_tiles(c, s):
                act.activation(sel[:, s, :].rearrange("p (q r) -> p q r", r=R), each(identb[:, bass.ds(c * TPC, TPC)], R),
                               ACT.Copy).then_inc(sel_ready, 1)
            act.wait_ge(coef_consts, 1)
            for c in range(2):
                select_tiles(c, c)

            def copy_types(s):
                take(act, typ_ps)
                take(act, typ_s_free)
                act.activation(typ_s[:, s, :], flat(PS[:, 2 * s:2 * s + 2, :])[:, 0:NB * TILE], ACT.Copy).then_inc(typ_s_ready, 1)
            with act.Fori(1, NK // 2) as i:
                for s in range(2):
                    copy_types(s)
                    select_tiles(2 * i + s, s)
            copy_types(0)
            copy_types(1)

            act.wait_ge(x_in, 32)

            def add_messages(g, h, use):
                for k in range(CPG):
                    if k == 0:
                        if not (isinstance(g, int) and g in (0, NG - 1)):
                            take(act, ix_free)
                            act.activation(ix[:, 1 - h, :], srcT[:, bass.ds((g + 1) * TPG, TPG)], ACT.Copy).then_inc(ix_ready, 1)
                        act.activation(xn[:, h, 0:D], win(X, g), ACT.Copy).then_inc(xwin_ready, 1)
                    take(act, z_ready)
                    act.activation(zs[:, k % 2, :, :, :].rearrange("p (a q) k n -> p a (q k n)", a=2),
                                   PS[:, 2 * (k % 2):2 * (k % 2) + 2, 0:2 * ZW], ACT.Copy).then_inc(z_copied, 1)
                    if k == 2:
                        take(act, xwT_ps)
                        act.activation(xT[:, h, 0:D], PS[:, 7, 0:P], ACT.Copy).then_inc(xwT_ready, 1)
            by_pairs(act, NG, add_messages)

            def turned_sums(bias):
                def copy_sums(u, s, use):
                    if not first_use(use):
                        take(act, accw_ps)
                    act.activation(xT[:, s, :], ACC[:, bass.ds(u * (WPB * TNODES), WPB * TNODES)], ACT.Identity,
                                   bias=bias).then_inc(accw_ready, 1)
                by_pairs(act, NBU, copy_sums)
                take(act, accw_ps, 2)

            act.wait_ge(wts_in, 16 * 10)
            take(act, sums_done)
            turned_sums(bn_in[:, 4:5])
            take(act, var_ready)
            act.activation(ln_r[:, :], ln_mv[:, :, 1], ACT.Sqrt).then_inc(sd_ready, 1)

            def copy_b(u, s, use):
                take(act, nT_ps)
                act.activation(xT[:, s, :], PS[:, 2 + s, :], ACT.Copy).then_inc(nT_ready, 1)
                take(act, b_ps)
                if not first_use(use):
                    reached(act, "act", bst_out[s], 16 * use)
                act.activation(bst[:, s, :], PS[:, 6 + s, :], ACT.Copy).then_inc(act_self, 1)
                take(act, act_self)
                act.sem_inc(bst_ready, 1)
                act.sem_inc(b_copied, 1)
            act.sem_inc(b_copied, 2)
            by_pairs(act, NBU, copy_b)

            for h in range(2):
                take(act, ix_free)
                act.activation(ix[:, h, :], srcT[:, h * TPG:(h + 1) * TPG], ACT.Copy).then_inc(ix_ready, 1)
            act.sem_inc(e_free, 2)

            def store_e(g, h, use):
                if not first_use(use):
                    reached(act, "act", stored[h], 16 * use)
                    take(act, e_measured)
                for k in range(CPG):
                    take(act, e_ready)
                    act.activation(stage[:, h, k * CHUNK:(k + 1) * CHUNK], PS[:, 2 + k % 2, :],
                                   ACT.Copy).then_inc(act_self, 1)
                    take(act, act_self)
                    act.sem_inc(e_free, 1)
                    act.sem_inc(e_copied, 1)
                act.dma_start(spill[bass.ds(g, 1), :, :].rearrange("o p n -> (o p) n"), stage[:, h, :]).then_inc(stored[h], 16)
                if not isinstance(g, int) or g + 2 < NG:
                    take(act, ix_free)
                    act.activation(ix[:, h, :], srcT[:, bass.ds((g + 2) * TPG, TPG)], ACT.Copy).then_inc(ix_ready, 1)
            store_e(0, 0, 0)
            store_e(1, 1, 0)
            with act.Fori(1, NG // 2 - 1) as i:
                store_e(2 * i, 0, i)
                store_e(2 * i + 1, 1, i)
            for g in range(NG - 3, NG):
                store_e(g, g % 2, g // 2)
            take(act, e_measured, 2)
            act.sem_inc(st_free, 2)
            act.sem_inc(hot_free, 2)

            def deviation(at):
                take(act, bn_var)
                act.activation(small[:, at + 3:at + 4], small[:, at + 2:at + 3], ACT.Sqrt).then_inc(bn_sd, 1)
            deviation(0)
            act.wait_ge(bn0_ready, 1)

            def relu_e(g, h, use):
                reached(act, "act", st_in[h], 16 * (use + 1))
                take(act, hot_free)
                act.activation(hot[:, h, :], stage[:, h, :], ACT.Relu, bias=small[:, 6:7],
                               scale=small[:, 5:6]).then_inc(hot_ready, 1)
            by_pairs(act, NG, relu_e)
            deviation(8)
            act.wait_ge(pass3_go, 1)

            def relu_e_again(g, h, use, k):
                if k == 0:
                    reached(act, "act", st_in[h], 16 * (use + 1 + (EVEN, ODD)[h]))
                c = slice(k * CHUNK, (k + 1) * CHUNK)
                act.activation(hot[:, h, c], stage[:, h, c], ACT.Relu, bias=small[:, 6:7],
                               scale=small[:, 5:6]).then_inc(hot_ready, 1)

            def relu_e2(g, h, use):
                for k in range(CPG):
                    if not last(g, NG):
                        relu_e_again(g + 1, 1 - h, use + h, k)
                    take(act, y_ready)
                    take(act, r2_free)
                    act.activation(R2[:, k, :, :].rearrange("p q d -> p (q d)"), PS[:, k, :],
                                   ACT.Relu).then_inc(r2_ready, 1)
            for k in range(CPG):
                relu_e_again(0, 0, 0, k)
            by_pairs(act, NG, relu_e2)

            turned_sums(0.0)
            take(act, var_ready)
            act.activation(ln_r[:, :], ln_mv[:, :, 1], ACT.Sqrt).then_inc(sd_ready, 1)

        @block.vector
        def _(dve):
            def step(ins):
                ins.then_inc(dve_self, 1)
                take(dve, dve_self)

            dve.wait_ge(const_done, 9)
            step(dve.tensor_copy(p_int[:, 0:1], node_col[:, 0:1]))
            step(dve.tensor_scalar(p_int[:, 1:2], p_int[:, 0:1], R.bit_length() - 1, None, ALU.arith_shift_right))
            step(dve.scalar_tensor_tensor(out=rel_col[:, :], in0=p_int[:, 1:2], scalar=-float(R), in1=p_int[:, 0:1],
                                          op0=ALU.mult, op1=ALU.add))
            step(dve.tensor_copy(identb[:, :], ident[:, :]))
            dve.wait_ge(edges_in["dst"], 48)
            step(dve.tensor_copy(f_dst, r_dst))
            step(dve.tensor_scalar(f_min, f_dst, 0.0, float(1 << 13), ALU.is_lt, ALU.mult))
            step(dve.tensor_tensor(f_min, f_min, f_dst, ALU.add))
            step(dve.tensor_reduce(t_min, f_min, AX.X, ALU.min))
            step(dve.tensor_reduce(t_max, f_dst, AX.X, ALU.max))
            dve.sem_inc(minmax, 1)
            step(dve.tensor_scalar(t_first, t_min, float(N - 1), None, ALU.min))
            step(dve.tensor_tensor(f_rel0, f_dst, each(t_first, TILE), ALU.subtract))
            dve.sem_inc(rel0_rows, 1)
            take(dve, minmax_T)
            dve.tensor_reduce(c_max, PS[0:NB, 0, P:2 * P].rearrange("b (c t) -> b c t", t=TPC), AX.X, ALU.max)
            step(dve.tensor_reduce(c_min, PS[0:NB, 0, 0:P].rearrange("b (c t) -> b c t", t=TPC), AX.X, ALU.min))
            step(dve.tensor_copy(c_tile.rearrange("b (c t) -> b c t", t=TPC), each(c_min, TPC)))
            dve.sem_inc(base_rows, 1)
            step(dve.tensor_tensor(c_max, c_max, c_min, ALU.subtract))
            step(dve.tensor_copy(c_ext[:, 0:NK], c_max))
            assert WIN == 16 * 5 and N <= 16 * 1023
            step(dve.tensor_scalar(c_ext[:, NK:2 * NK], c_ext[:, 0:NK], 4, None, ALU.arith_shift_right))
            step(dve.tensor_scalar(c_ext[:, 0:NK], c_ext[:, NK:2 * NK], 205.0, None, ALU.mult))
            step(dve.tensor_scalar(c_ext[:, NK:2 * NK], c_ext[:, 0:NK], 10, None, ALU.arith_shift_right))
            step(dve.tensor_scalar(c_min, c_min, float(SPAN), None, ALU.add))
            step(dve.scalar_tensor_tensor(out=c_win, in0=c_ext[:, NK:2 * NK], scalar=float(SPAN), in1=c_min,
                                          op0=ALU.mult, op1=ALU.add))
            dve.sem_inc(setup_out, 1)
            take(dve, base_T)
            step(dve.tensor_copy(t_base, PS[:, 1, 0:NB]))
            step(dve.tensor_tensor(f_rel, f_dst, each(t_base, TILE), ALU.subtract))
            dve.sem_inc(rel_rows, 1)
            assert TWIN == 8 * 3 and N <= 8 * 1023
            step(dve.tensor_scalar(e_min, PS[0:NB, 0, 0:P], float(N - 1), None, ALU.min))
            step(dve.tensor_tensor(e_ext, PS[0:NB, 0, P:2 * P], e_min, ALU.subtract))
            step(dve.tensor_scalar(e_int[:, 0:P], e_ext, 0.0, None, ALU.max))
            step(dve.tensor_scalar(e_int[:, P:2 * P], e_int[:, 0:P], 3, None, ALU.arith_shift_right))
            step(dve.tensor_scalar(e_int[:, 0:P], e_int[:, P:2 * P], 683.0, None, ALU.mult))
            step(dve.tensor_scalar(e_int[:, P:2 * P], e_int[:, 0:P], 11, None, ALU.arith_shift_right))
            step(dve.tensor_copy(e_ext, e_int[:, P:2 * P]))
            step(dve.tensor_reduce(e_wide, e_ext.rearrange("b (g t) -> b g t", t=TPG), AX.X, ALU.max))
            step(dve.tensor_copy(e_pair, e_min))
            step(dve.tensor_scalar(e_min, e_min, float(SPAN), None, ALU.add))
            step(dve.scalar_tensor_tensor(out=e_reach, in0=e_ext, scalar=float(SPAN), in1=e_min, op0=ALU.mult, op1=ALU.add))
            dve.sem_inc(setup_out, 1)
            step(dve.tensor_copy(i_rel, f_rel))
            step(dve.tensor_scalar(i_hi, i_rel, TNODES_BITS, None, ALU.arith_shift_right))
            dve.tensor_scalar(dig_hi, i_hi, float(TNODES), None, ALU.mult)
            step(dve.scalar_tensor_tensor(out=dig_lo, in0=i_hi, scalar=-float(TNODES), in1=i_rel, op0=ALU.mult, op1=ALU.add))
            dve.sem_inc(setup_out, 1)
            step(dve.tensor_scalar(a_hi, r_dst, TNODES_BITS, None, ALU.arith_shift_right))
            step(dve.tensor_copy(f_hi, a_hi))
            dve.sem_inc(hi_rows, 1)
            step(dve.scalar_tensor_tensor(out=f_lo, in0=f_hi, scalar=-float(TNODES), in1=f_dst, op0=ALU.mult, op1=ALU.add))
            dve.sem_inc(lo_rows, 1)
            dve.wait_ge(wcomp_in, 16 * TPC)
            for a in range(3):
                step(dve.tensor_copy(wbd_p[:, a, :], wbd if a == 0 else wbd_r))
                if a < 2:
                    step(dve.tensor_tensor(wbd_r, wbd if a == 0 else wbd_r, wbd_p[:, a, :], ALU.subtract))
            dve.sem_inc(coef_consts, 1)
            dve.wait_ge(wT_ps, 1)
            step(dve.tensor_copy(thph[:, 0:D], PS[:, 6, 0:D]))
            step(dve.tensor_copy(fc1T[:, :], PS[:, 6, 2 * D:3 * D]))
            step(dve.tensor_tensor(thph[:, D:2 * D], PS[:, 6, D:2 * D], thph[:, 0:D], ALU.subtract))
            dve.wait_ge(cols_ready, 6)
            dve.wait_ge(typ_rows, 1)
            step(dve.memset(X[:, NW - 1:NWP, :], 0.0))
            dve.sem_inc(rows_used, 1)
            dve.sem_inc(wT_done, 1)

            dve.sem_inc(coef_free, 2)
            dve.sem_inc(typ_s_free, 2)

            def one_hot_types(s):
                take(dve, typ_s_ready)
                dve.tensor_scalar(rel_oh[:, s, :], typ_s[:, s, :], rel_col[:, :], None, ALU.is_equal).then_inc(rel_oh_ready, 1)

            def scale_coef(c, s):
                tiles = bass.ds(c * TPC, TPC)
                nrm = normT[:, :].rearrange("p (b t o) -> p b t o", b=NB, o=1)[:, :, tiles, :].to_broadcast([P, NB, TPC, B])
                take(dve, coef_ps)
                dve.sem_inc(typ_s_free, 1)
                dve.tensor_tensor(coef[:, :, tiles, :],
                                  PS[:, 4 + s, 0:NB * TPC * B].rearrange("p (b q k) -> p b q k", b=NB, q=TPC),
                                  nrm, ALU.mult).then_inc(coef_free, 1)
            one_hot_types(0)
            with dve.Fori(0, NK // 2 - 1) as i:
                one_hot_types(1)
                scale_coef(2 * i, 0)
                one_hot_types(0)
                scale_coef(2 * i + 1, 1)
            one_hot_types(1)
            scale_coef(NK - 2, 0)
            scale_coef(NK - 1, 1)
            dve.drain().then_inc(dve_self, 1)
            take(dve, dve_self)

            dve.wait_ge(bnd_in, 64)

            def add_sums(g, k, bank):
                reach = reach_of(dve, CPG * g + k)
                base = least_dst(dve, reach)
                acc = ACC[:, bass.ds(base, WIN)]
                take(dve, added)
                dve.sem_inc(seg_free, 1)
                take(dve, seg_ready)
                dve.tensor_tensor(acc, acc, PS[:, bank + k % 2, 0:WIN], ALU.add).then_inc(added, 1)

                def further(i):
                    for q in range(TPC):
                        t = TPG * g + TPC * k + q
                        step(dve.tensor_scalar(ohx[:, q, :], iota_w[:, 0:WIN], win_off[:, bass.ds(i, 1)],
                                               dstT[:, bass.ds(t, 1)], ALU.add, ALU.is_equal))
                    dve.sem_inc(ohx_ready, 1)
                    take(dve, segx_ready)
                    accx = ACC[:, bass.ds(nc.s_assert_within(base + i * WIN, 0, N - 1, skip_runtime_bounds_check_because="no window starts past the greatest dst"), WIN)]
                    take(dve, added)
                    dve.tensor_tensor(accx, accx, PS[:, bank + 2, 0:WIN], ALU.add).then_inc(added, 1)
                further_windows(dve, reach, further)

            coefs = coef.rearrange("p b t k -> p (b t k)")

            def scaled_hot(g, k, q):
                t = TPG * g + TPC * k + q
                ins = dve.scalar_tensor_tensor(out=soh[:, k, q, :, :], in0=over(iota_w[:, 0:TWIN], B, TWIN),
                                               scalar=dst0T[:, bass.ds(t, 1)], in1=each(coefs[:, bass.ds(t * B, B)], TWIN),
                                               op0=ALU.is_equal, op1=ALU.mult)
                if q == TPC - 1:
                    ins.then_inc(oh_ready, 1)

            def add_messages(g, h, use):
                def tile(j, reach):
                    t = TPG * g + j
                    take(dve, added)
                    step(dve.tensor_copy(gx, G[:, h, bass.ds(j, 1), :].rearrange("p o d -> p (o d)")))

                    def further(i):
                        step(dve.tensor_scalar(ohx[:, 0, 0:TWIN], iota_w[:, 0:TWIN], win_off0[:, bass.ds(i, 1)],
                                               dst0T[:, bass.ds(t, 1)], ALU.add, ALU.is_equal))
                        step(dve.tensor_tensor(sohx, over(ohx[:, 0, 0:TWIN], B, TWIN), each(coefs[:, bass.ds(t * B, B)], TWIN), ALU.mult))
                        dve.sem_inc(ohx_ready, 1)
                        take(dve, zx_ready)
                        step(dve.tensor_copy(zsx.rearrange("p k n -> p (k n)"), PS[:, 6, 0:ZW]))
                        dve.sem_inc(zx_copied, 1)
                        take(dve, segx_ready)
                        accx = ACC[:, bass.ds(nc.s_assert_within(reach % SPAN + i * TWIN, 0, N - 1, skip_runtime_bounds_check_because="no window starts past the greatest dst"), TWIN)]
                        step(dve.tensor_tensor(accx, accx, PS[:, 6, ZW:ZW + TWIN], ALU.add))
                    further_windows(dve, reach, further)
                    dve.sem_inc(added, 1)
                tile_windows(dve, g, tile, lambda: take(dve, group_in))
                for k in range(CPG):
                    firsts = pair_of(dve, TPG * g + TPC * k)
                    take(dve, added)
                    dve.sem_inc(seg_free, 1)
                    if k == 0:
                        dve.sem_inc(loop_done, 1)
                    firsts += pair_of(dve, TPG * g + TPC * k + 2)
                    accs = [ACC[:, bass.ds(b, TWIN)] for b in firsts]
                    nxt = after(g, h, use, k)
                    nxt = nxt and after(*nxt)
                    nxt = nxt and after(*nxt)
                    take(dve, seg_ready)
                    dve.sem_inc(g_free, 1)
                    for q in range(TPC):
                        if q > 0:
                            take(dve, added)
                        dve.tensor_tensor(accs[q], accs[q], PS[:, 4 + k % 2, q * TWIN:(q + 1) * TWIN], ALU.add).then_inc(added, 1)
                        if nxt:
                            scaled_hot(nxt[0], nxt[3], q)
                acc = ACC[:, bass.ds(g * TNODES, TNODES)]
                take(dve, loop_ps)
                take(dve, added)
                dve.tensor_tensor(acc, acc, PS[:, 7, P:2 * P], ALU.add).then_inc(added, 1)


            dve.sem_inc(seg_free, 1)
            take(dve, acc_zero)
            dve.sem_inc(added, 1)
            for k in range(3):
                for q in range(TPC):
                    scaled_hot(0, k, q)
            by_pairs(dve, NG, add_messages)
            take(dve, added)
            take(dve, seg_free)
            dve.sem_inc(sums_done, 1)

            def moments(u):
                for w in range(WPB):
                    dve.bn_stats(win(ln_st, u * WPB + w), win(X, u * WPB + w))

            def layer_norm_stats():
                dve.drain()
                m0, m1, v0, v1 = ln_st[:, :, 1], ln_st[:, :, 4], ln_st[:, :, 2], ln_st[:, :, 5]
                step(dve.tensor_tensor(ln_mv[:, :, 0], m0, m1, ALU.add))
                step(dve.tensor_scalar(ln_mv[:, :, 0], ln_mv[:, :, 0], 0.5, None, ALU.mult))
                step(dve.tensor_tensor(ln_mv[:, :, 1], m0, m1, ALU.subtract))
                step(dve.tensor_scalar(ln_mv[:, :, 1], ln_mv[:, :, 1], 0.5, None, ALU.mult))
                step(dve.tensor_tensor(ln_mv[:, :, 1], ln_mv[:, :, 1], ln_mv[:, :, 1], ALU.mult))
                step(dve.tensor_tensor(ln_r[:, :], v0, v1, ALU.add))
                step(dve.scalar_tensor_tensor(out=ln_mv[:, :, 1], in0=ln_r[:, :], scalar=1.0 / D, in1=ln_mv[:, :, 1],
                                              op0=ALU.mult, op1=ALU.add))
                step(dve.tensor_scalar(ln_mv[:, :, 1], ln_mv[:, :, 1], EPS, None, ALU.add))
                dve.sem_inc(var_ready, 1)
                take(dve, sd_ready)
                step(dve.reciprocal(ln_r[:, :], ln_r[:, :]))

            def normalise(u, s):
                for w in range(WPB):
                    v = u * WPB + w
                    ins = dve.tensor_scalar(xn[:, s, w * D:(w + 1) * D], win(X, v), ln_mv[:, bass.ds(v, 1), 0],
                                            ln_r[:, bass.ds(v, 1)], ALU.subtract, ALU.mult)
                return ins

            dve.sem_inc(accw_used, 2)

            def residual0(u, s, use):
                take(dve, sums_turned)
                dve.sem_inc(accw_ps, 1)
                xb = flat(X[:, bass.ds(u * WPB, WPB), :])
                step(dve.scalar_tensor_tensor(out=xb, in0=PS[:, s, :], scalar=0.0, in1=xb, op0=ALU.max, op1=ALU.add))
                dve.sem_inc(accw_used, 1)
                moments(u)
            by_pairs(dve, NBU, residual0)
            layer_norm_stats()

            dve.sem_inc(a_split, 2)
            dve.sem_inc(xn_free, 2)

            def send_normal(u, s, use):
                take(dve, xn_free)
                step(normalise(u, s))
                dve.sem_inc(xn_kept, 1)
                dve.sem_inc(xn_ready, 1)

            def split_a(u, s, use):
                if not last(u, NBU):
                    send_normal(u + 1, 1 - s, use + s)
                take(dve, a_ps)
                if not first_use(use):
                    reached(dve, "dve", ast_out[s], 16 * use)
                ps = PS[:, 4 + s, :].rearrange("p (w d) -> p w d", w=WPB)
                res = resid[:, :].rearrange("p (w d) -> p w d", w=WPB)
                hi, mid, low = (ast[:, s, :, a, :] for a in range(3))
                step(dve.tensor_copy(hi, ps))
                step(dve.tensor_tensor(res, ps, hi, ALU.subtract))
                dve.sem_inc(a_split, 1)
                step(dve.tensor_copy(mid, res))
                step(dve.tensor_tensor(low, res, mid, ALU.subtract))
                dve.sem_inc(ast_ready, 1)
            send_normal(0, 0, 0)
            by_pairs(dve, NBU, split_a)
            take(dve, xn_free, 2)

            def count_hots(g, k):
                tiles = bass.ds(TPG * g + TPC * k, TPC)
                take(dve, cnt_done)
                dve.tensor_tensor(oh_lo[:, k % 2, :, :], over(iota_w[:, :], TPC, TNODES), each(loT[:, tiles], TNODES), ALU.is_equal)
                dve.tensor_tensor(oh_hi[:, k % 2, :, :], over(iota_h[:, :], TPC, NW), each(hiT[:, tiles], NW),
                                  ALU.is_equal).then_inc(cnt_oh, 1)

            dve.sem_inc(cnt_done, 2)
            dve.sem_inc(dig_free, 2)
            dve.sem_inc(d_free, 2)
            dve.sem_inc(aw_free, CPG)
            dve.sem_inc(awx_free, 1)

            def look_up(k):
                take(dve, d_ready)
                dve.tensor_scalar(ohT[0:WIN, k % 2, :], PS[0:WIN, k % 2, :], node_col[0:WIN, 0:1], None, ALU.is_equal).then_inc(ohT_ready, 1)

            def first_moments(g, h, k):
                c = CPG * g + k
                take(dve, e_copied)
                cols = LASTC if last(c, NCH) else CHUNK
                dve.bn_stats(win(stats, c), stage[:, h, k * CHUNK:k * CHUNK + cols])

            def edge_features(g, h, use):
                for k in range(CPG):
                    nxt = after(g, h, use, k)
                    if nxt:
                        look_up(nxt[3])
                        count_hots(nxt[0], nxt[3])
                    reach = reach_of(dve, CPG * g + k)
                    take(dve, look_done)

                    def further(i):
                        dve.tensor_scalar(ohTx[0:WIN, :], PS[0:WIN, k % 2, :], node_col[0:WIN, bass.ds(i, 1)], None,
                                          ALU.is_equal).then_inc(ohTx_ready, 1)
                        take(dve, lookx_done)
                        dve.sem_inc(awx_free, 1)
                    further_windows(dve, reach, further)
                    for s in (d_free, g_free, aw_free, e_ready):
                        dve.sem_inc(s, 1)
                    if k == CPG - 1:
                        dve.sem_inc(dig_free, 1)
                        dve.sem_inc(ix_free, 1)
                    if k >= 1:
                        first_moments(g, h, k - 1)
                first_moments(g, h, CPG - 1)
                dve.drain().then_inc(e_measured, 1)
            look_up(0)
            count_hots(0, 0)
            by_pairs(dve, NG, edge_features)
            take(dve, cnt_done, 2)
            step(dve.memset(rcnt[:, :], 1.0))
            step(dve.tensor_scalar(rcnt[:, 0:NW], PS[:, 7, 0:NW], 1.0, None, ALU.max))
            step(dve.reciprocal(rcnt[:, :], rcnt[:, :]))

            def scale_and_shift(at, g, b):
                dve.drain()
                step(dve.bn_aggr(small[:, at + 1:at + 3], flat(stats[:, :, :])))
                step(dve.tensor_scalar(small[:, at + 2:at + 3], small[:, at + 2:at + 3], EPS, None, ALU.add))
                dve.sem_inc(bn_var, 1)
                take(dve, bn_sd)
                step(dve.reciprocal(small[:, at + 4:at + 5], small[:, at + 3:at + 4]))
                step(dve.tensor_tensor(small[:, at + 5:at + 6], small[:, at + 4:at + 5], bn_in[:, g:g + 1], ALU.mult))
                step(dve.tensor_tensor(small[:, at + 7:at + 8], small[:, at + 1:at + 2], small[:, at + 5:at + 6], ALU.mult))
                step(dve.tensor_tensor(small[:, at + 6:at + 7], bn_in[:, b:b + 1], small[:, at + 7:at + 8], ALU.subtract))

            dve.memset(shift3[:, :, :], 0.0)
            scale_and_shift(0, 0, 1)
            dve.sem_inc(e2_free, 2 * CPG)
            dve.sem_inc(bn0_ready, 1)

            def second_moments(g, h, use):
                for k in range(CPG):
                    c = CPG * g + k
                    take(dve, e2_ready)
                    cols = LASTC if last(c, NCH) else CHUNK
                    dve.bn_stats(win(stats, c), PS[:, CPG * h + k, 0:cols]).then_inc(e2_free, 1)
                dve.sem_inc(hot_free, 1)
            by_pairs(dve, NG, second_moments)
            dve.wait_ge(e2_free, 2 * CPG)
            scale_and_shift(8, 2, 3)
            step(dve.tensor_scalar(diag[:, :], fc1_s[:, :], small[:, 13:14], None, ALU.mult))
            step(dve.tensor_scalar(diag_t[:, :], ident[:, :], small[:, 14:15], None, ALU.mult))
            dve.sem_inc(fc1_scaled, 1)
            take(dve, acc_zero)
            take(dve, fc1s_ps)
            step(dve.tensor_copy(fc1sT[:, :], PS[:, 0, 0:D]))
            shift_all, rest = resid[:, 0:D], resid[:, D:2 * D]
            part_all = oh_lo[:, 0, 0, :]
            step(dve.tensor_copy(shift_all, PS[:, 1, 0:D]))
            for a in range(3):
                step(dve.tensor_copy(part_all, shift_all))
                row = slice(32 * a, 32 * a + 1)
                step(dve.tensor_copy(shift3[row, :, :], part_all[row, :].rearrange("p (o d) -> p o d", o=1).to_broadcast([1, TPC, D])))
                if a < 2:
                    step(dve.tensor_tensor(rest, shift_all, part_all, ALU.subtract))
                    step(dve.tensor_copy(shift_all, rest))
            dve.sem_inc(r2_free, CPG)
            dve.sem_inc(oh_free, CPG)
            dve.sem_inc(pass3_go, 1)

            def sum_edges(g, h, use):
                for k in range(CPG):
                    add_sums(g, k, 4)
                    dve.sem_inc(r2_free, 1)
                    dve.sem_inc(oh_free, 1)
            dve.sem_inc(seg_free, 1)
            dve.sem_inc(added, 1)
            by_pairs(dve, NG, sum_edges)
            take(dve, added)

            def residual1(u, s, use):
                take(dve, sums_turned)
                dve.sem_inc(accw_ps, 1)
                for w in range(WPB):
                    v = u * WPB + w
                    ins = dve.scalar_tensor_tensor(out=resid[:, w * D:(w + 1) * D], in0=PS[:, s, w * D:(w + 1) * D],
                                                   scalar=rcnt[:, bass.ds(v, 1)], in1=win(X, v), op0=ALU.mult, op1=ALU.add)
                step(ins)
                dve.sem_inc(accw_used, 1)
                xb = flat(X[:, bass.ds(u * WPB, WPB), :])
                step(dve.scalar_tensor_tensor(out=xb, in0=resid[:, :], scalar=0.0, in1=xb, op0=ALU.max, op1=ALU.add))
                moments(u)
            by_pairs(dve, NBU, residual1)
            layer_norm_stats()

            def result(u, s, use):
                if not first_use(use):
                    reached(dve, "dve", res_out[s], 16 * use)
                normalise(u, s).then_inc(res_ready, 1)
            by_pairs(dve, NBU, result)


_INS = ['x', 'src', 'dst', 'edge_type_32', 'edge_weight1', 'L0_gnn_weight', 'L0_gnn_w_comp', 'L0_gnn_loop_weight',
        'L0_gnn_h_bias', 'L1_gnn_theta_w', 'L1_gnn_phi_w', 'L1_gnn_fc1_w', 'L1_gnn_bn0_g', 'L1_gnn_bn0_b',
        'L1_gnn_bn1_g', 'L1_gnn_bn1_b']


def kernel(**inputs):
    import numpy as np
    import concourse.bacc as bacc
    from concourse.bass_utils import run_bass_kernel_spmd as run

    nc = bacc.Bacc("TRN2", target_bir_lowering=False, num_devices=1)
    arrays, args = {}, []
    for name in _INS:
        a = np.ascontiguousarray(inputs[name])
        arrays[f"in_{name}"] = a
        args.append(nc.dram_tensor(f"in_{name}", a.shape, mybir.dt.from_np(a.dtype), kind="ExternalInput").ap())
    out = nc.dram_tensor("out_0", inputs["x"].shape, F32, kind="ExternalOutput").ap()
    gnn_kernel(nc, *args, out)
    return run(nc, [arrays], core_ids=[0]).results[0]["out_0"]
```
